# Optimizing a Trainium2 kernel written in Bass

```python
import numpy as np
import jax
import jax.numpy as jnp

def _softmax(x, axis=-1):
    return jax.nn.softmax(x, axis=axis)

def _gelu(x):
    return jax.nn.gelu(x, approximate=True)

def _silu(x):
    return jax.nn.silu(x)

def _sigmoid(x):
    return jax.nn.sigmoid(x)

def _layernorm(x, axis=-1, eps=1e-05):
    m = jnp.mean(x, axis=axis, keepdims=True)
    v = jnp.var(x, axis=axis, keepdims=True)
    return (x - m) / jnp.sqrt(v + eps)

def _scatter_add(tgt, idx, src, axis=0):
    return tgt.at[idx].add(src)

def _segment_sum(src, seg, n):
    return jax.ops.segment_sum(src, seg, n)
kernel_name = 'mk_xattn_ffn_d1_seqx_r8_95a137'

def setup_inputs(seed: int=0):
    np.random.seed(seed)
    _w = jnp.asarray

    def _rec_inputs():
        import jax
        import jax.numpy as jnp
        _rk = jax.random.key(seed)
        x = -0.0002928 + 1 * jax.random.normal(jax.random.fold_in(_rk, 1), (4, 256, 128), jnp.float32)
        _lenS = 256 - jax.random.randint(jax.random.fold_in(_rk, 7), (4,), 0, max(1, 256 // 4) + 1, jnp.int32)
        _lenS2 = 64 - jax.random.randint(jax.random.fold_in(_rk, 8), (4,), 0, max(1, 64 // 4) + 1, jnp.int32)
        _ctx_1024P = jax.random.normal(jax.random.fold_in(_rk, 11), (4, 16, 128), jnp.float32)
        _ctx_1024c = jax.random.dirichlet(jax.random.fold_in(_rk, 511), 0.3 * jnp.ones((16,), jnp.float32), (4, 64))
        _ctx_1024t = jnp.einsum('bsk,bkd->bsd', _ctx_1024c, _ctx_1024P)
        _ctx_1024t = _ctx_1024t * jax.lax.rsqrt(jnp.mean(jnp.square(_ctx_1024t)) + 1e-12) * 0.953939
        ctx_1024 = -1.39393e-06 + 0.999914 * (_ctx_1024t + 0.3 * jax.random.normal(jax.random.fold_in(_rk, 611), (4, 64, 128), jnp.float32))
        return (x, ctx_1024)
    x, ctx_1024 = _rec_inputs()

    def _L0_xattn_setup():
        import jax, jax.numpy as jnp
        import numpy as np
        HEADS = 16
        DIM_HEAD = 64
        QUERY_DIM = 128
        INNER = HEADS * DIM_HEAD
        SCALE = DIM_HEAD ** (-0.5)
        key = jax.random.key(seed)
        ks = jax.random.split(key, 6)
        B, N, M = (2, 256, 256)
        x = jax.random.normal(ks[0], (B, N, QUERY_DIM), dtype=jnp.float32)
        context = jax.random.normal(ks[1], (B, M, QUERY_DIM), dtype=jnp.float32)
        s = QUERY_DIM ** (-0.5)
        Wq = jax.random.normal(ks[2], (QUERY_DIM, INNER), dtype=jnp.float32) * s
        Wk = jax.random.normal(ks[3], (QUERY_DIM, INNER), dtype=jnp.float32) * s
        Wv = jax.random.normal(ks[4], (QUERY_DIM, INNER), dtype=jnp.float32) * s
        Wo = jax.random.normal(ks[5], (INNER, QUERY_DIM), dtype=jnp.float32) * INNER ** (-0.5)
        return {'x': x, 'context': context, 'Wq': Wq, 'Wk': Wk, 'Wv': Wv, 'Wo': Wo}
    _L0_xattn_all = _L0_xattn_setup()
    _L0_xattn_in = {k: v for k, v in _L0_xattn_all.items() if k in ('Wq', 'Wk', 'Wv', 'Wo')}
    del _L0_xattn_all

    def _L0_ffn_setup():
        import jax, jax.numpy as jnp
        import numpy as np
        TOP_K = 2
        key = jax.random.key(seed)
        k1, k2, k3 = jax.random.split(key, 3)
        B, S, H, E, D = (4, 128, 128, 32, 128)
        x = jax.random.normal(k1, (B, S, H), dtype=jnp.float32)
        router_w = jax.random.normal(k2, (E, H), dtype=jnp.float32) * (1.0 / np.sqrt(H))
        bound = float(np.sqrt(6.0 / ((1.0 + 0.01 ** 2) * H)))
        expert_weights = jax.random.uniform(k3, (E, H, D), dtype=jnp.float32, minval=-bound, maxval=bound)
        return {'x': x, 'router_w': router_w, 'expert_weights': expert_weights}
    _L0_ffn_all = _L0_ffn_setup()
    _L0_ffn_in = {k: v for k, v in _L0_ffn_all.items() if k in ('router_w', 'expert_weights')}
    del _L0_ffn_all
    return {'x': x, 'ctx_1024': ctx_1024, 'L0_xattn_Wq': _L0_xattn_in['Wq'], 'L0_xattn_Wk': _L0_xattn_in['Wk'], 'L0_xattn_Wv': _L0_xattn_in['Wv'], 'L0_xattn_Wo': _L0_xattn_in['Wo'], 'L0_ffn_router_w': _L0_ffn_in['router_w'], 'L0_ffn_expert_weights': _L0_ffn_in['expert_weights']}

def reference(x, ctx_1024, L0_xattn_Wq, L0_xattn_Wk, L0_xattn_Wv, L0_xattn_Wo, L0_ffn_router_w, L0_ffn_expert_weights):
    import jax
    import jax.numpy as jnp

    def _L0_xattn_ref(x, context, Wq, Wk, Wv, Wo):
        import jax, jax.numpy as jnp
        import numpy as np
        HEADS = 16
        DIM_HEAD = 64
        QUERY_DIM = 128
        INNER = HEADS * DIM_HEAD
        SCALE = DIM_HEAD ** (-0.5)
        B, N, _ = x.shape
        M = context.shape[1]
        q = (x @ Wq).reshape(B, N, HEADS, DIM_HEAD)
        k = (context @ Wk).reshape(B, M, HEADS, DIM_HEAD)
        v = (context @ Wv).reshape(B, M, HEADS, DIM_HEAD)
        sim = jnp.einsum('bihd,bjhd->bhij', q, k) * SCALE
        attn = jax.nn.softmax(sim, axis=-1)
        out = jnp.einsum('bhij,bjhd->bihd', attn, v)
        out = out.reshape(B, N, INNER)
        return out @ Wo

    def _L0_ffn_ref(x, router_w, expert_weights):
        import jax, jax.numpy as jnp
        import numpy as np
        TOP_K = 2
        B, S, H = x.shape
        E = router_w.shape[0]
        T = B * S
        logits = jnp.einsum('bsh,eh->bse', x, router_w)
        rw = jax.nn.softmax(logits, axis=-1).reshape(T, E)
        x_flat = x.reshape(T, H)
        vals, idx = jax.lax.top_k(rw, TOP_K)
        w_masked = jnp.zeros_like(rw).at[jnp.arange(T)[:, None], idx].set(vals)

        def body(acc, we):
            w_e, W_e = we
            return (acc + x_flat * w_e[:, None] @ W_e, None)
        out_flat, _ = jax.lax.scan(body, jnp.zeros((T, H), dtype=x.dtype), (w_masked.T, expert_weights))
        return out_flat.reshape(B, S, H)
    x = x + _L0_xattn_ref(_layernorm(x, axis=-1), ctx_1024, L0_xattn_Wq, L0_xattn_Wk, L0_xattn_Wv, L0_xattn_Wo)
    x = x + _L0_ffn_ref(_layernorm(x, axis=-1), L0_ffn_router_w, L0_ffn_expert_weights)
    return x

_drawn_inputs = setup_inputs


def setup_inputs(seed=0):
    import zlib

    import numpy as np

    out = dict(_drawn_inputs(seed))
    spreads = {}
    factors = {}
    for name, (base, spread) in spreads.items():
        noise = np.random.default_rng([zlib.crc32(name.encode()), seed]).standard_normal(out[name].shape)
        drawn = base * np.exp(spread * noise) if base else spread * noise
        out[name] = jnp.asarray(drawn.astype(out[name].dtype))
    for name, factor in factors.items():
        out[name] = (out[name] * factor).astype(out[name].dtype)
    return out
```

```python
from contextlib import ExitStack

import numpy as np

import concourse.bass as bass
from concourse import mybir

F32 = mybir.dt.float32
F32R = mybir.dt.float32r
U32 = mybir.dt.uint32
ALU = mybir.AluOpType
ACT = mybir.ActivationFunctionType
AX = mybir.AxisListType

P = 128
B, N, D = 4, 256, 128
M = 64
H, DH = 16, 64
E = 32
NT = B * N // P
TB = N // P
C = H * DH // P
BANK = 512
EB = BANK // D
EC = E // EB
EPS = 1e-5
SCALE = DH ** -0.5
DVE_CHUNKS = (0, 2, 4, 6, 7)
ACT_CHUNKS = tuple(c for c in range(EC) if c not in DVE_CHUNKS)
ND, NA = len(DVE_CHUNKS), len(ACT_CHUNKS)
FB = 3


def build(nc, x, ctxT, wk, wqT, wv, wo, rwT, we, ident_d, sel_d, iota_d, out):
    with ExitStack() as ctx:
        def sb(name, shape, dt=F32):
            return ctx.enter_context(nc.sbuf_tensor(name, shape, dt))

        def sem(name):
            return ctx.enter_context(nc.semaphore(name))

        x_in = sb("x_in", [P, NT, D])
        ctx_t = sb("ctx_t", [P, B * M])
        wk_sb = sb("wk_sb", [P, H * DH])
        wq_sb = sb("wq_sb", [P, C, P])
        wv_sb = sb("wv_sb", [P, H * DH])
        wo_sb = sb("wo_sb", [P, C, D])
        rw_sb = sb("rw_sb", [P, E])
        we_sb = sb("we_sb", [P, E * D])
        we_hi = sb("we_hi", [P, E * D], F32R)
        we_lo = sb("we_lo", [P, E * D], F32R)
        ident = sb("ident", [P, P])
        sel_in = sb("sel_in", [2 * H, H * M])
        sel = sb("sel", [2 * H, H * M], F32R)
        iota = sb("iota", [P, E])
        kt_bd = sb("kt_bd", [P, C, 2, B * M])
        vt_bd = sb("vt_bd", [P, C, B, 2 * M])
        g_hi = sb("g_hi", [P, B, H, M], F32R)
        g_lo = sb("g_lo", [P, B, H, M], F32R)
        u_sb = sb("u_sb", [P, B, C, D])
        yt_hi = sb("yt_hi", [P, NT, P], F32R)
        yt_lo = sb("yt_lo", [P, NT, P], F32R)
        mhalf = sb("mhalf", [P, NT])
        st1 = sb("st1", [P, NT, 6])
        mv1 = sb("mv1", [P, NT, 2])
        ve1 = sb("ve1", [P, NT])
        rstd1 = sb("rstd1", [P, NT])
        nmax = sb("nmax", [P, 2, H])
        nmax_hl = sb("nmax_hl", [P, 2, 2 * H], F32R)
        nmaxT = sb("nmaxT", [2 * H, 2, P], F32R)
        prob = sb("prob", [P, 2, H, M])
        psum_h = sb("psum_h", [P, 2, H])
        rsum_h = sb("rsum_h", [P, 2, H])
        at = sb("at", [P, 2, C, P])
        x1 = sb("x1", [P, NT, D])
        st2 = sb("st2", [P, NT, 6])
        mv2 = sb("mv2", [P, NT, 2])
        ve2 = sb("ve2", [P, NT])
        rstd2 = sb("rstd2", [P, NT])
        xn = sb("xn", [P, 2, D])
        xt = sb("xt", [P, 2, P])
        xt_hi = sb("xt_hi", [P, 2, P], F32R)
        xt_lo = sb("xt_lo", [P, 2, P], F32R)
        lg = sb("lg", [P, 2, E])
        top8 = sb("top8", [P, 2, 8])
        ntop = sb("ntop", [P, 2, 1])
        idx8 = sb("idx8", [P, 2, 8], U32)
        idxf = sb("idxf", [P, 2, 2])
        m1 = sb("m1", [P, 2, E])
        m12 = sb("m12", [P, 2, E])
        el = sb("el", [P, 2, E])
        es = sb("es", [P, 2, 1])
        er = sb("er", [P, 2, 1])
        wt = sb("wt", [P, 2, E])
        acc = sb("acc", [P, 2, D])
        abuf = sb("abuf", [P, 3, BANK])
        pacc = sb("pacc", [P, 2, BANK])
        pfold = sb("pfold", [P, 2, 2 * D])
        o_sb = x_in
        y_sb = x1

        bank = [ctx.enter_context(nc.psum_tensor(f"bank{n}", [P, BANK], F32)) for n in range(2, 8)]
        sim = ctx.enter_context(nc.psum_tensor("sim", [P, 2 * BANK], F32))
        attn_ps, misc_ps, av_ps = bank[0], bank[1], bank[2]
        ffn_ps = bank[3:6]
        kt_ps = [sim[:, 0:BANK], sim[:, BANK:2 * BANK], bank[0][:, :], bank[1][:, :]]
        g_ps = [b[:, :] for b in bank[2:6]]

        ld = {n: sem(f"ld_{n}") for n in ("ctx", "wk", "x0", "x1", "wq", "ident", "sel", "iota", "wv", "wo", "rw")}
        ld_we = [sem(f"ld_we{n}") for n in range(4)]
        out_stored = sem("out_stored")
        zero_k = sem("zero_k")
        zero_v = sem("zero_v")
        consts = sem("consts")
        sel_ready = sem("sel_ready")
        k_ready = sem("k_ready")
        k_act = sem("k_act")
        k_dve = sem("k_dve")
        g_ready = sem("g_ready")
        g_hi_ready = sem("g_hi_ready")
        g_lo_ready = sem("g_lo_ready")
        v_ready = sem("v_ready")
        v_act = sem("v_act")
        v_dve = sem("v_dve")
        u_ready = sem("u_ready")
        u_copied = sem("u_copied")
        dve_stats1 = sem("dve_stats1")
        ve1_ready = sem("ve1_ready")
        rstd1_ready = sem("rstd1_ready")
        y_ready = sem("y_ready")
        yt_ready = sem("yt_ready")
        yt_hi_ready = sem("yt_hi_ready")
        yt_lo_ready = sem("yt_lo_ready")
        we_hi_ready = sem("we_hi_ready")
        we_lo_ready = sem("we_lo_ready")
        sim_ready = sem("sim_ready")
        nmax_done = sem("nmax_done")
        nmax_hi_done = sem("nmax_hi_done")
        nmax_ready = sem("nmax_ready")
        nmaxT_ready = sem("nmaxT_ready")
        nmaxT_copied = sem("nmaxT_copied")
        fold_ready = sem("fold_ready")
        exp_done = sem("exp_done")
        sum_done = sem("sum_done")
        rsum_ready = sem("rsum_ready")
        norm_done = sem("norm_done")
        attnT_ready = sem("attnT_ready")
        attnT_copied = sem("attnT_copied")
        av_ready = sem("av_ready")
        x1_done = sem("x1_done")
        dve_stats2 = sem("dve_stats2")
        ve2_ready = sem("ve2_ready")
        rstd2_ready = sem("rstd2_ready")
        xn_ready = sem("xn_ready")
        xnT_ready = sem("xnT_ready")
        xt_ready = sem("xt_ready")
        xt_hi_done = sem("xt_hi_done")
        xt_split = sem("xt_split")
        logits_ready = sem("logits_ready")
        logits_copied = sem("logits_copied")
        top_done = sem("top_done")
        ntop_ready = sem("ntop_ready")
        idx_done = sem("idx_done")
        el_ready = sem("el_ready")
        er_done = sem("er_done")
        w_ready = sem("w_ready")
        ffn_ready = sem("ffn_ready")
        acc_step = sem("acc_step")
        act_weighed = sem("act_weighed")
        pool_added = sem("pool_added")
        pool_folded = sem("pool_folded")
        acc_merged = sem("acc_merged")
        merge_in = sem("merge_in")

        block = ctx.enter_context(nc.Block())

        def in_dve(k):
            return k // EC * ND + sum(c < k % EC for c in DVE_CHUNKS)

        def in_act(k):
            return k - in_dve(k)

        @block.sync
        def _(sp):
            sp.dma_start(ctx_t[:, :], ctxT).then_inc(ld["ctx"], 16)
            sp.dma_start(wk_sb[:, :], wk).then_inc(ld["wk"], 16)
            sp.dma_start(wq_sb[:, :, :], wqT).then_inc(ld["wq"], 16)
            sp.dma_start(sel_in[:, :], sel_d).then_inc(ld["sel"], 16)
            sp.dma_start(wv_sb[:, :], wv).then_inc(ld["wv"], 16)
            sp.dma_start(wo_sb[:, :, :], wo).then_inc(ld["wo"], 16)
            sp.dma_start(rw_sb[:, :], rwT).then_inc(ld["rw"], 16)
            sp.dma_start(iota[:, :], iota_d).then_inc(ld["iota"], 16)
            for n in range(4):
                w = slice(n * E * D // 4, (n + 1) * E * D // 4)
                sp.dma_start(we_sb[:, w], we[:, w]).then_inc(ld_we[n], 16)
            for j in range(NT):
                sp.wait_ge(acc_merged, j + 1)
                sp.dma_start(out[:, j, :], o_sb[:, j, :]).then_inc(out_stored, 16)
            sp.wait_ge(out_stored, 16 * NT)

        @block.tensor
        def _(pe):
            def k_pair(j):
                for c in (2 * j, 2 * j + 1):
                    mm = nc.tensor.matmul(kt_ps[j][:, (c % 2) * B * M:(c % 2 + 1) * B * M],
                                          wk_sb[:, c * P:(c + 1) * P], ctx_t[:, :], start=True, stop=True)
                mm.then_inc(k_ready, 1)

            def g_pair(c):
                if c % 2 == 0:
                    pe.wait_ge(k_act, c // 2 + 1)
                    pe.wait_ge(k_dve, c // 2 + 1)
                if c >= 4:
                    pe.wait_ge(g_lo_ready, c - 3)
                nc.tensor.matmul(g_ps[c % 4], wq_sb[:, c, :], kt_bd[:, c, :, :], start=True,
                                 stop=True).then_inc(g_ready, 1)

            def y_turn(q):
                pe.wait_ge(y_ready, 4 * (q + 1))
                for t in range(4):
                    mm = nc.tensor.transpose(sim[:, q * BANK + t * P:q * BANK + (t + 1) * P],
                                             y_sb[:, 4 * q + t, :], ident[:, :])
                mm.then_inc(yt_ready, 1)

            def scores(i):
                b = i // TB
                if i:
                    pe.wait_ge(exp_done, i)
                else:
                    pe.wait_ge(yt_lo_ready, 2)
                    pe.wait_ge(g_lo_ready, C)
                for s in range(2):
                    hs = slice(s * H // 2, (s + 1) * H // 2)
                    o = sim[:, s * BANK:(s + 1) * BANK]
                    nc.tensor.matmul(o, yt_hi[:, i, :], g_hi[:, b, hs, :], start=True, stop=False)
                    nc.tensor.matmul(o, yt_hi[:, i, :], g_lo[:, b, hs, :], start=False, stop=False)
                    mm = nc.tensor.matmul(o, yt_lo[:, i, :], g_hi[:, b, hs, :], start=False, stop=True)
                mm.then_inc(sim_ready, 1)

            def turn_max(i):
                pe.wait_ge(nmax_ready, i + 1)
                if i >= 2:
                    pe.wait_ge(logits_copied, i - 1)
                nc.tensor.transpose(misc_ps[0:2 * H, 0:P], nmax_hl[:, i % 2, :].bitcast(F32),
                                    ident[:, :]).then_inc(nmaxT_ready, 1)

            def subtract_max(i):
                pe.wait_ge(nmaxT_copied, i + 1)
                if i == 0:
                    pe.wait_ge(sel_ready, 1)
                for s in range(2):
                    mm = nc.tensor.matmul(sim[:, s * BANK:(s + 1) * BANK], nmaxT[:, i % 2, :],
                                          sel[:, s * BANK:(s + 1) * BANK], start=False, stop=True,
                                          skip_group_check=True)
                mm.then_inc(fold_ready, 1)

            def v_pair(j):
                pe.wait_ge(g_lo_ready, C)
                if j == 3:
                    pe.wait_ge(v_act, 1)
                    pe.wait_ge(v_dve, 1)
                for c in (2 * j, 2 * j + 1):
                    mm = nc.tensor.matmul(ffn_ps[j % FB][:, (c % 2) * B * M:(c % 2 + 1) * B * M],
                                          wv_sb[:, c * P:(c + 1) * P], ctx_t[:, :], start=True, stop=True)
                mm.then_inc(v_ready, 1)

            def u_half(n):
                b, half = n // 2, n % 2
                if n == 0:
                    pe.wait_ge(v_act, 4)
                    pe.wait_ge(v_dve, 4)
                    pe.wait_ge(ld["wo"], 16)
                if n >= FB:
                    pe.wait_ge(u_copied, n - FB + 1)
                for q in range(4):
                    c = 4 * half + q
                    mm = nc.tensor.matmul(ffn_ps[n % FB][:, q * D:(q + 1) * D], vt_bd[:, c, b, :],
                                          wo_sb[:, c, :], start=True, stop=True)
                mm.then_inc(u_ready, 1)

            def turn_attn(i, half):
                if half == 0:
                    pe.wait_ge(norm_done, i + 1)
                if 2 * i + half >= 1:
                    pe.wait_ge(attnT_copied, 2 * i + half)
                for q in range(4):
                    c = 4 * half + q
                    mm = nc.tensor.transpose(attn_ps[:, q * P:(q + 1) * P],
                                             prob[:, i % 2, 2 * c:2 * c + 2, :], ident[:, :])
                mm.then_inc(attnT_ready, 1)

            def attend(i):
                pe.wait_ge(attnT_copied, 2 * i + 2)
                if i:
                    pe.wait_ge(x1_done, i)
                if i % TB == 0:
                    pe.wait_ge(u_copied, 2 * (i // TB) + 2)
                for c in range(C):
                    mm = nc.tensor.matmul(av_ps[:, 0:D], at[:, i % 2, c, :], u_sb[:, i // TB, c, :],
                                          start=(c == 0), stop=(c == C - 1))
                mm.then_inc(av_ready, 1)

            def turn_xn(i):
                pe.wait_ge(xn_ready, i + 1)
                if i:
                    pe.wait_ge(logits_copied, i)
                nc.tensor.transpose(misc_ps[:, P:2 * P], xn[:, i % 2, :], ident[:, :]).then_inc(xnT_ready, 1)

            def router(i):
                pe.wait_ge(xt_ready, i + 1)
                if i == 0:
                    pe.wait_ge(ld["rw"], 16)
                nc.tensor.matmul(misc_ps[:, 2 * P:2 * P + E], xt[:, i % 2, :], rw_sb[:, :],
                                 start=True, stop=True).then_inc(logits_ready, 1)

            def experts(j, c):
                k = EC * j + c
                if c == 0:
                    pe.wait_ge(xt_split, j + 1)
                if k == 0:
                    pe.wait_ge(u_copied, 2 * B)
                    pe.wait_ge(we_hi_ready, 4)
                if k < EC and k % 2 == 0:
                    pe.wait_ge(we_lo_ready, k // 2 + 1)
                if k >= FB:
                    if (k - FB) % EC in DVE_CHUNKS:
                        pe.wait_ge(acc_step, EB * in_dve(k - FB + 1))
                    else:
                        pe.wait_ge(act_weighed, in_act(k - FB + 1))
                o = ffn_ps[k % FB][:, :]
                w = slice(c * BANK, (c + 1) * BANK)
                nc.tensor.matmul(o, xt_hi[:, j % 2, :], we_hi[:, w], start=True, stop=False)
                nc.tensor.matmul(o, xt_hi[:, j % 2, :], we_lo[:, w], start=False, stop=False)
                nc.tensor.matmul(o, xt_lo[:, j % 2, :], we_hi[:, w], start=False,
                                 stop=True).then_inc(ffn_ready, 1)

            pe.wait_ge(ld["ctx"], 16)
            pe.wait_ge(ld["wk"], 16)
            for j in range(4):
                k_pair(j)
            pe.wait_ge(ld["wq"], 16)
            for c in range(C):
                g_pair(c)
            pe.wait_ge(ld["ident"], 16)
            for q in range(2):
                y_turn(q)
            for i in range(NT + 2):
                j = i - 2
                def F(*cs):
                    if j >= 0:
                        for c in cs:
                            experts(j, c)
                live, prev = i < NT, 0 <= i - 1 < NT
                if live:
                    scores(i)
                F(0, 1)
                if i == 0:
                    pe.wait_ge(ld["wv"], 16)
                    for n in range(4):
                        v_pair(n)
                if prev:
                    turn_attn(i - 1, 0)
                if live:
                    turn_max(i)
                F(2)
                if prev:
                    turn_attn(i - 1, 1)
                if live:
                    subtract_max(i)
                if i == 0:
                    for n in range(4):
                        u_half(n)
                F(3)
                if prev:
                    attend(i - 1)
                F(4, 5)
                if i == 1:
                    for n in range(4, 8):
                        u_half(n)
                if prev:
                    turn_xn(i - 1)
                F(6)
                if prev:
                    router(i - 1)
                F(7)

        @block.vector
        def _(dve):
            def layer_norm_1():
                for t in range(NT):
                    if t % 4 == 0:
                        dve.wait_ge(ld[f"x{t // 4}"], 16)
                    nc.vector.bn_stats(st1[:, t, :], x_in[:, t, :]).then_inc(dve_stats1, 1)
                for t in range(NT):
                    dve.wait_ge(dve_stats1, t + 1)
                    nc.vector.bn_aggr(mv1[:, t, :], st1[:, t, :]).then_inc(dve_stats1, 1)
                dve.wait_ge(dve_stats1, 2 * NT)
                nc.vector.tensor_scalar(ve1[:, :], mv1[:, :, 1], EPS, None, ALU.add).then_inc(ve1_ready, 1)

            def apply_norm_1():
                dve.wait_ge(rstd1_ready, 1)
                for t in range(NT):
                    nc.vector.tensor_scalar(y_sb[:, t, :], x_in[:, t, :], mv1[:, t, 0:1], rstd1[:, t:t + 1],
                                            ALU.subtract, ALU.mult).then_inc(y_ready, 1)

            def k_copy(j):
                dve.wait_ge(k_ready, j + 1)
                nc.vector.tensor_copy(kt_bd[M:P, 2 * j:2 * j + 2, 1, :],
                                      kt_ps[j][M:P, :].rearrange("p (c n) -> p c n", c=2)).then_inc(k_dve, 1)

            def g_rest(c):
                dve.wait_ge(g_hi_ready, c + 1)
                nc.vector.tensor_tensor(g_lo[:, :, 2 * c:2 * c + 2, :],
                                        g_ps[c % 4].rearrange("p (h b k) -> p b h k", h=2, b=B),
                                        g_hi[:, :, 2 * c:2 * c + 2, :].bitcast(F32),
                                        ALU.subtract).then_inc(g_lo_ready, 1)

            def y_rest(q):
                dve.wait_ge(yt_hi_ready, q + 1)
                nc.vector.tensor_tensor(yt_lo[:, 4 * q:4 * q + 4, :],
                                        sim[:, q * BANK:(q + 1) * BANK].rearrange("p (t n) -> p t n", t=4),
                                        yt_hi[:, 4 * q:4 * q + 4, :].bitcast(F32),
                                        ALU.subtract).then_inc(yt_lo_ready, 1)

            def v_copy(j):
                dve.wait_ge(v_ready, j + 1)
                nc.vector.tensor_copy(vt_bd[M:P, 2 * j:2 * j + 2, :, M:2 * M],
                                      ffn_ps[j % FB][M:P, :].rearrange("p (c b k) -> p c b k", c=2, b=B)
                                      ).then_inc(v_dve, 1)

            def row_max(i):
                dve.wait_ge(sim_ready, i + 1)
                nc.vector.tensor_reduce(nmax[:, i % 2, :], sim[:, :].rearrange("p (h k) -> p h k", h=H),
                                        AX.X, ALU.max, negate=True).then_inc(nmax_done, 1)
                dve.wait_ge(nmax_done, i + 1)
                if i >= 2:
                    dve.wait_ge(nmaxT_ready, i - 1)
                nc.vector.tensor_copy(nmax_hl[:, i % 2, 0:H], nmax[:, i % 2, :]).then_inc(nmax_hi_done, 1)
                dve.wait_ge(nmax_hi_done, i + 1)
                nc.vector.tensor_tensor(nmax_hl[:, i % 2, H:2 * H], nmax[:, i % 2, :],
                                        nmax_hl[:, i % 2, 0:H].bitcast(F32), ALU.subtract).then_inc(nmax_ready, 1)

            def copy_maxT(i):
                dve.wait_ge(nmaxT_ready, i + 1)
                if i >= 2:
                    dve.wait_ge(fold_ready, i - 1)
                nc.vector.tensor_copy(nmaxT[:, i % 2, :], misc_ps[0:2 * H, 0:P]).then_inc(nmaxT_copied, 1)

            def row_sum(i):
                dve.wait_ge(exp_done, i + 1)
                nc.vector.tensor_reduce(psum_h[:, i % 2, :], prob[:, i % 2, :, :], AX.X, ALU.add).then_inc(sum_done, 1)
                dve.wait_ge(sum_done, i + 1)
                if i >= 2:
                    dve.wait_ge(norm_done, i - 1)
                nc.vector.reciprocal(rsum_h[:, i % 2, :], psum_h[:, i % 2, :]).then_inc(rsum_ready, 1)

            def residual(i):
                dve.wait_ge(av_ready, i + 1)
                nc.vector.tensor_tensor(x1[:, i, :], av_ps[:, 0:D], x_in[:, i, :], ALU.add).then_inc(x1_done, 1)
                dve.wait_ge(x1_done, i + 1)
                nc.vector.bn_stats(st2[:, i, :], x1[:, i, :]).then_inc(dve_stats2, 1)
                dve.wait_ge(dve_stats2, 2 * i + 1)
                nc.vector.bn_aggr(mv2[:, i, :], st2[:, i, :]).then_inc(dve_stats2, 1)
                dve.wait_ge(dve_stats2, 2 * i + 2)
                nc.vector.tensor_scalar(ve2[:, i:i + 1], mv2[:, i, 1:2], EPS, None, ALU.add).then_inc(ve2_ready, 1)

            def normalise(i):
                dve.wait_ge(rstd2_ready, i + 1)
                if i >= 2:
                    dve.wait_ge(xnT_ready, i - 1)
                nc.vector.tensor_scalar(xn[:, i % 2, :], x1[:, i, :], mv2[:, i, 0:1], rstd2[:, i:i + 1],
                                        ALU.subtract, ALU.mult).then_inc(xn_ready, 1)

            def split_xt(i):
                dve.wait_ge(xt_ready, i + 1)
                if i >= 2:
                    dve.wait_ge(ffn_ready, EC * (i - 1))
                nc.vector.tensor_copy(xt_hi[:, i % 2, :], xt[:, i % 2, :]).then_inc(xt_hi_done, 1)
                dve.wait_ge(xt_hi_done, i + 1)
                nc.vector.tensor_tensor(xt_lo[:, i % 2, :], xt[:, i % 2, :], xt_hi[:, i % 2, :].bitcast(F32),
                                        ALU.subtract).then_inc(xt_split, 1)

            def top_two(i):
                p = i % 2
                dve.wait_ge(logits_ready, i + 1)
                nc.vector.tensor_copy(lg[:, p, :], misc_ps[:, 2 * P:2 * P + E]).then_inc(logits_copied, 1)
                dve.wait_ge(logits_copied, i + 1)
                nc.vector.max(top8[:, p, :], lg[:, p, :]).then_inc(top_done, 1)
                dve.wait_ge(top_done, i + 1)
                nc.vector.tensor_scalar(ntop[:, p, :], top8[:, p, 0:1], -1.0, None, ALU.mult).then_inc(ntop_ready, 1)
                nc.vector.max_index(idx8[:, p, :], top8[:, p, :], lg[:, p, :]).then_inc(idx_done, 1)
                dve.wait_ge(idx_done, 4 * i + 1)
                nc.vector.tensor_copy(idxf[:, p, :], idx8[:, p, 0:2]).then_inc(idx_done, 1)
                dve.wait_ge(idx_done, 4 * i + 2)
                nc.vector.tensor_scalar(m1[:, p, :], iota[:, :], idxf[:, p, 0:1], None, ALU.is_equal).then_inc(idx_done, 1)
                dve.wait_ge(idx_done, 4 * i + 3)
                nc.vector.scalar_tensor_tensor(m12[:, p, :], iota[:, :], idxf[:, p, 1:2], m1[:, p, :],
                                               ALU.is_equal, ALU.add).then_inc(idx_done, 1)

            def weights(i):
                p = i % 2
                dve.wait_ge(el_ready, i + 1)
                nc.vector.reciprocal(er[:, p, :], es[:, p, :]).then_inc(er_done, 1)
                dve.wait_ge(er_done, i + 1)
                dve.wait_ge(idx_done, 4 * i + 4)
                if i >= 2:
                    dve.wait_ge(act_weighed, NA * (i - 1))
                nc.vector.scalar_tensor_tensor(wt[:, p, :], el[:, p, :], er[:, p, 0:1], m12[:, p, :],
                                               ALU.mult, ALU.mult).then_inc(w_ready, 1)

            def weigh(j, c):
                k = EC * j + c
                dve.wait_ge(ffn_ready, k + 1)
                for q in range(EB):
                    e = EB * c + q
                    n = EB * in_dve(k) + q
                    first = n % (EB * ND)
                    if first == 0:
                        if j == 0:
                            dve.wait_ge(w_ready, 1)
                        before = x1[:, j, :]
                    elif first == 1:
                        before = None
                    else:
                        before = acc[:, n % 2, :]
                    if first < 2 and j:
                        dve.wait_ge(acc_merged, j)
                    if first >= 2:
                        dve.wait_ge(acc_step, n - 1)
                    y = ffn_ps[k % FB][:, q * D:(q + 1) * D]
                    w = wt[:, j % 2, e:e + 1]
                    if before is None:
                        ins = nc.vector.tensor_scalar(acc[:, n % 2, :], y, w, None, ALU.mult)
                    else:
                        ins = nc.vector.scalar_tensor_tensor(acc[:, n % 2, :], y, w, before, ALU.mult, ALU.add)
                    ins.then_inc(acc_step, 1)

            def merge(j):
                dve.wait_ge(acc_step, EB * ND * (j + 1))
                dve.wait_ge(pool_folded, 2 * (j + 1))
                nc.vector.tensor_tensor(acc[:, 0, :], acc[:, 0, :], acc[:, 1, :], ALU.add).then_inc(merge_in, 1)
                dve.wait_ge(merge_in, j + 1)
                nc.vector.tensor_tensor(o_sb[:, j, :], acc[:, 0, :], pfold[:, 1, 0:D], ALU.add).then_inc(acc_merged, 1)

            for half in range(2):
                (nc.vector.memset(vt_bd[0:M, :, :, M:2 * M], 0.0) if half == 0 else
                 nc.vector.memset(vt_bd[M:P, :, :, 0:M], 0.0)).then_inc(zero_v, 1)
            layer_norm_1()
            dve.wait_ge(zero_k, 2)
            for j in range(4):
                k_copy(j)
            for c in range(4):
                g_rest(c)
            apply_norm_1()
            for c in range(4, C):
                g_rest(c)
            dve.wait_ge(ld["sel"], 16)
            nc.vector.tensor_copy(sel[:, :], sel_in[:, :]).then_inc(sel_ready, 1)
            for q in range(2):
                y_rest(q)
            dve.wait_ge(ld["iota"], 16)
            for i in range(NT + 2):
                j = i - 2
                def W(*cs):
                    if j >= 0:
                        for c in cs:
                            if c in DVE_CHUNKS:
                                weigh(j, c)
                live, prev = i < NT, 0 <= i - 1 < NT
                if live:
                    row_max(i)
                if i == 0:
                    for n in range(4):
                        v_copy(n)
                W(0, 1)
                if live:
                    copy_maxT(i)
                W(2)
                if i == 0:
                    for n in range(4):
                        dve.wait_ge(ld_we[n], 16)
                        w = slice(n * E * D // 4, (n + 1) * E * D // 4)
                        nc.vector.tensor_copy(we_hi[:, w], we_sb[:, w]).then_inc(we_hi_ready, 1)
                if live:
                    row_sum(i)
                W(3)
                if prev:
                    residual(i - 1)
                W(4, 5)
                if prev:
                    normalise(i - 1)
                W(6)
                if prev:
                    split_xt(i - 1)
                    top_two(i - 1)
                W(7)
                if prev:
                    weights(i - 1)
                if j >= 0:
                    merge(j)

        @block.scalar
        def _(act):
            act.dma_start(x_in[:, 0:4, :], x[:, 0:4, :]).then_inc(ld["x0"], 16)
            act.dma_start(x_in[:, 4:8, :], x[:, 4:8, :]).then_inc(ld["x1"], 16)
            act.dma_start(ident[:, :], ident_d).then_inc(ld["ident"], 16)

            def k_copy(j):
                act.wait_ge(k_ready, j + 1)
                nc.scalar.activation(kt_bd[0:M, 2 * j:2 * j + 2, 0, :],
                                     kt_ps[j][0:M, :].rearrange("p (c n) -> p c n", c=2), ACT.Copy).then_inc(k_act, 1)

            def g_round(c):
                act.wait_ge(g_ready, c + 1)
                nc.scalar.activation(g_hi[:, :, 2 * c:2 * c + 2, :],
                                     g_ps[c % 4].rearrange("p (h b k) -> p b h k", h=2, b=B),
                                     ACT.Copy).then_inc(g_hi_ready, 1)

            def y_round(q):
                act.wait_ge(yt_ready, q + 1)
                nc.scalar.activation(yt_hi[:, 4 * q:4 * q + 4, :],
                                     sim[:, q * BANK:(q + 1) * BANK].rearrange("p (t n) -> p t n", t=4),
                                     ACT.Copy).then_inc(yt_hi_ready, 1)

            def v_copy(j):
                act.wait_ge(v_ready, j + 1)
                nc.scalar.activation(vt_bd[0:M, 2 * j:2 * j + 2, :, 0:M],
                                     ffn_ps[j % FB][0:M, :].rearrange("p (c b k) -> p c b k", c=2, b=B),
                                     ACT.Copy).then_inc(v_act, 1)

            def u_copy(n):
                act.wait_ge(u_ready, n + 1)
                nc.scalar.activation(u_sb[:, n // 2, 4 * (n % 2):4 * (n % 2) + 4, :],
                                     ffn_ps[n % FB][:, :].rearrange("p (c d) -> p c d", c=4),
                                     ACT.Copy).then_inc(u_copied, 1)

            def exponentials(i):
                act.wait_ge(fold_ready, i + 1)
                if i >= 2:
                    act.wait_ge(attnT_ready, 2 * (i - 1))
                nc.scalar.activation(prob[:, i % 2, :, :], sim[:, :].rearrange("p (h k) -> p h k", h=H),
                                     ACT.Exp, scale=SCALE).then_inc(exp_done, 1)

            def attnT_copy(i, half):
                act.wait_ge(attnT_ready, 2 * i + half + 1)
                if i >= 2:
                    act.wait_ge(av_ready, i - 1)
                nc.scalar.activation(at[:, i % 2, 4 * half:4 * half + 4, :],
                                     attn_ps[:, :].rearrange("p (c n) -> p c n", c=4),
                                     ACT.Copy).then_inc(attnT_copied, 1)

            def xt_copy(i):
                act.wait_ge(xnT_ready, i + 1)
                if i >= 2:
                    act.wait_ge(xt_split, i - 1)
                    act.wait_ge(logits_ready, i - 1)
                nc.scalar.activation(xt[:, i % 2, :], misc_ps[:, P:2 * P], ACT.Copy).then_inc(xt_ready, 1)

            def router_exp(i):
                act.wait_ge(ntop_ready, i + 1)
                if i >= 2:
                    act.wait_ge(w_ready, i - 1)
                nc.scalar.activation(el[:, i % 2, :], lg[:, i % 2, :], ACT.Exp, bias=ntop[:, i % 2, 0:1],
                                     accum_out=es[:, i % 2, 0:1]).then_inc(el_ready, 1)

            def weigh(j, c):
                k = EC * j + c
                n = in_act(k)
                act.wait_ge(ffn_ready, k + 1)
                act.wait_ge(w_ready, j + 1)
                if n >= 3:
                    act.wait_ge(pool_added, (NA - 1) * ((n - 3) // NA) + max((n - 3) % NA, 1))
                for q in range(EB):
                    e = EB * c + q
                    ins = nc.scalar.activation(abuf[:, n % 3, q * D:(q + 1) * D],
                                               ffn_ps[k % FB][:, q * D:(q + 1) * D], ACT.Copy,
                                               scale=wt[:, j % 2, e:e + 1])
                ins.then_inc(act_weighed, 1)

            act.wait_ge(zero_k, 2)
            for j in range(4):
                k_copy(j)
            for c in range(C):
                g_round(c)
            for q in range(2):
                y_round(q)
            for i in range(NT + 2):
                j = i - 2
                def W(*cs):
                    if j >= 0:
                        for c in cs:
                            if c in ACT_CHUNKS:
                                weigh(j, c)
                live, prev = i < NT, 0 <= i - 1 < NT
                if i == 0:
                    act.wait_ge(zero_v, 2)
                    for n in range(4):
                        v_copy(n)
                W(0, 1)
                if prev:
                    attnT_copy(i - 1, 0)
                W(2)
                if prev:
                    attnT_copy(i - 1, 1)
                if live:
                    exponentials(i)
                if i == 0:
                    for n in range(4):
                        u_copy(n)
                W(3, 4, 5)
                if i == 1:
                    for n in range(4, 8):
                        u_copy(n)
                if prev:
                    xt_copy(i - 1)
                W(6)
                if prev:
                    router_exp(i - 1)
                W(7)

        @block.gpsimd
        def _(pool):
            nc.gpsimd.memset(kt_bd[0:M, :, 1, :], 0.0).then_inc(zero_k, 1)
            pool.wait_ge(zero_k, 1)
            nc.gpsimd.memset(kt_bd[M:P, :, 0, :], 0.0).then_inc(zero_k, 1)
            pool.wait_ge(zero_k, 2)
            nc.gpsimd.memset(mhalf[:, :], -0.5).then_inc(consts, 1)
            pool.wait_ge(consts, 1)
            pool.wait_ge(ve1_ready, 1)
            nc.gpsimd.tensor_tensor(rstd1[:, :], ve1[:, :], mhalf[:, :], ALU.pow).then_inc(rstd1_ready, 1)

            def we_rest(n):
                pool.wait_ge(we_hi_ready, n + 1)
                w = slice(n * E * D // 4, (n + 1) * E * D // 4)
                nc.gpsimd.tensor_tensor(we_lo[:, w], we_sb[:, w], we_hi[:, w].bitcast(F32),
                                        ALU.subtract).then_inc(we_lo_ready, 1)

            def normalise_probs(i):
                pool.wait_ge(rsum_ready, i + 1)
                nc.gpsimd.tensor_tensor(prob[:, i % 2, :, :], prob[:, i % 2, :, :],
                                        rsum_h[:, i % 2, :].unsqueeze(2).broadcast_to([P, H, M]),
                                        ALU.mult).then_inc(norm_done, 1)

            def rstd(i):
                pool.wait_ge(ve2_ready, i + 1)
                nc.gpsimd.tensor_tensor(rstd2[:, i:i + 1], ve2[:, i:i + 1], mhalf[:, 0:1],
                                        ALU.pow).then_inc(rstd2_ready, 1)

            def gather(j, c):
                k = EC * j + c
                n = in_act(k)
                m = n % NA
                pool.wait_ge(act_weighed, n + 1)
                if m == 0:
                    return
                if m == 1:
                    if j:
                        pool.wait_ge(pool_folded, 2 * j)
                    first = abuf[:, (n - 1) % 3, :]
                else:
                    pool.wait_ge(pool_added, (NA - 1) * j + m - 1)
                    first = pacc[:, m % 2, :]
                ins = nc.gpsimd.tensor_tensor(pacc[:, (m + 1) % 2, :], first, abuf[:, n % 3, :], ALU.add)
                ins.then_inc(pool_added, 1)

            def fold(j):
                pool.wait_ge(pool_added, (NA - 1) * (j + 1))
                if j:
                    pool.wait_ge(acc_merged, j)
                a = pacc[:, NA % 2, :]
                nc.gpsimd.tensor_tensor(pfold[:, 0, :], a[:, 0:2 * D], a[:, 2 * D:4 * D], ALU.add).then_inc(pool_folded, 1)
                pool.wait_ge(pool_folded, 2 * j + 1)
                nc.gpsimd.tensor_tensor(pfold[:, 1, 0:D], pfold[:, 0, 0:D], pfold[:, 0, D:2 * D],
                                        ALU.add).then_inc(pool_folded, 1)

            for i in range(NT + 2):
                j = i - 2
                def A(*cs):
                    if j >= 0:
                        for c in cs:
                            if c in ACT_CHUNKS:
                                gather(j, c)
                live, prev = i < NT, 0 <= i - 1 < NT
                if i == 0:
                    for n in range(2):
                        we_rest(n)
                A(0, 1, 2)
                if live:
                    normalise_probs(i)
                if i == 0:
                    for n in range(2, 4):
                        we_rest(n)
                A(3)
                if prev:
                    rstd(i - 1)
                A(4, 5, 6, 7)
                if j >= 0:
                    fold(j)


_OUT = (B, N, D)


def kernel(**inputs):
    import concourse.bacc as _bacc
    from concourse.bass_utils import run_bass_kernel_spmd as _run

    a = {k: np.asarray(v) for k, v in inputs.items()}
    laid = {
        "x": a["x"].reshape(NT, P, D).transpose(1, 0, 2),
        "ctxT": a["ctx_1024"].reshape(B * M, D).T,
        "wk": a["L0_xattn_Wk"],
        "wqT": a["L0_xattn_Wq"].T.reshape(C, P, D).transpose(1, 0, 2),
        "wv": a["L0_xattn_Wv"],
        "wo": a["L0_xattn_Wo"].reshape(C, P, D).transpose(1, 0, 2),
        "rwT": a["L0_ffn_router_w"].T,
        "we": a["L0_ffn_expert_weights"].transpose(1, 0, 2).reshape(D, E * D),
        "ident": np.eye(P, dtype=np.float32),
        "sel": np.tile(np.repeat(np.eye(H, dtype=np.float32), M, axis=1), (2, 1)),
        "iota": np.tile(np.arange(E, dtype=np.float32), (P, 1)),
    }
    nc = _bacc.Bacc("TRN2", target_bir_lowering=False, num_devices=1)
    arrays, args = {}, []
    for name, v in laid.items():
        v = np.ascontiguousarray(v)
        arrays[f"in_{name}"] = v
        args.append(nc.dram_tensor(f"in_{name}", v.shape, mybir.dt.from_np(v.dtype), kind="ExternalInput").ap())
    args.append(nc.dram_tensor("out_0", (P, NT, D), F32, kind="ExternalOutput").ap())
    build(nc, *args)
    r = _run(nc, [arrays], core_ids=[0])
    got = r.results[0]["out_0"]
    return got.transpose(1, 0, 2).reshape(_OUT)
```

```python
from contextlib import ExitStack

import numpy as np

import concourse.bass as bass
from concourse import mybir

F32 = mybir.dt.float32
F32R = mybir.dt.float32r
U32 = mybir.dt.uint32
ALU = mybir.AluOpType
ACT = mybir.ActivationFunctionType
AX = mybir.AxisListType

P = 128
B, N, D = 4, 256, 128
M = 64
H, DH = 16, 64
E = 32
NT = B * N // P
TB = N // P
C = H * DH // P
BANK = 512
EB = BANK // D
EC = E // EB
EPS = 1e-5
SCALE = DH ** -0.5
DVE_CHUNKS = (1, 3, 5, 7)
ND, NA = len(DVE_CHUNKS), EC - len(DVE_CHUNKS)
DVE_MERGED = 3
LAST_DVE_CHUNKS = (1, 3, 5, 6, 7)
FB = 4
LAG = 3

FILLS = [(what, b, half) for what, b in (("K", 0), ("G", 0), ("V", 0), ("U", 0),
                                         ("K", 2), ("G", 1), ("V", 2), ("U", 1),
                                         ("G", 2), ("U", 2), ("G", 3), ("U", 3)) for half in range(2)]
assert len(FILLS) == LAG * EC and len(FILLS) % FB == 0


def dve_fills(n):
    return sum(what != "U" for what, _, _ in FILLS[:n])


def filled(what, b):
    return FILLS.index((what, b, 1)) + 1


def build(nc, x, ctxT, wk, wqT, wv, wo, rwT, we, ident_d, sel_d, iota_d, out):
    with ExitStack() as ctx:
        def sb(name, shape, dt=F32):
            return ctx.enter_context(nc.sbuf_tensor(name, shape, dt))

        def sem(name):
            return ctx.enter_context(nc.semaphore(name))

        x_in = sb("x_in", [P, NT, D])
        ctx_t = sb("ctx_t", [P, B, M])
        wk_sb = sb("wk_sb", [P, H * DH])
        wq_sb = sb("wq_sb", [P, C, P])
        wv_sb = sb("wv_sb", [P, H * DH])
        wo_sb = sb("wo_sb", [P, C, D])
        rw_sb = sb("rw_sb", [P, E])
        we_sb = sb("we_sb", [P, E * D])
        we_hi = sb("we_hi", [P, E * D], F32R)
        we_lo = sb("we_lo", [P, E * D], F32R)
        ident = sb("ident", [P, P])
        sel_in = sb("sel_in", [2 * H, H * M])
        sel = sb("sel", [2 * H, H * M], F32R)
        iota = sb("iota", [P, E])
        warm = sb("warm", [P, 1])
        kt_bd = sb("kt_bd", [P, C, B, 2 * M])
        vt_bd = sb("vt_bd", [P, C, B, 2 * M])
        g_hi = sb("g_hi", [P, B, H * M], F32R)
        g_lo = sb("g_lo", [P, B, H * M], F32R)
        u_sb = sb("u_sb", [P, B, C, D])
        yt_hi = sb("yt_hi", [P, NT, P], F32R)
        yt_lo = sb("yt_lo", [P, NT, P], F32R)
        mhalf = sb("mhalf", [P, NT])
        st1 = sb("st1", [P, NT, 6])
        mv1 = sb("mv1", [P, NT, 2])
        ve1 = sb("ve1", [P, NT])
        rstd1 = sb("rstd1", [P, NT])
        nmax = sb("nmax", [P, 2, H])
        nmax_hl = sb("nmax_hl", [P, 2, 2 * H], F32R)
        nmaxT = sb("nmaxT", [2 * H, 2, P], F32R)
        prob = sb("prob", [P, 2, H, M])
        psum_h = sb("psum_h", [P, 2, H])
        rsum_h = sb("rsum_h", [P, 2, H])
        at = sb("at", [P, 2, C, P])
        x1 = sb("x1", [P, NT, D])
        st2 = sb("st2", [P, NT, 6])
        mv2 = sb("mv2", [P, NT, 2])
        ve2 = sb("ve2", [P, NT])
        rstd2 = sb("rstd2", [P, NT])
        xn = sb("xn", [P, 2, D])
        xt = sb("xt", [P, 2, P])
        xt_hi = sb("xt_hi", [P, 2, P], F32R)
        xt_lo = sb("xt_lo", [P, 2, P], F32R)
        lg = sb("lg", [P, 2, E])
        top8 = sb("top8", [P, 2, 8])
        ntop = sb("ntop", [P, 2, 1])
        idx8 = sb("idx8", [P, 2, 8], U32)
        m1 = sb("m1", [P, 2, E])
        m12 = sb("m12", [P, 2, E])
        el = sb("el", [P, 2, E])
        es = sb("es", [P, 2, 1])
        er = sb("er", [P, 2, 1])
        wt = sb("wt", [P, 2, E])
        acc = sb("acc", [P, 2, 2, D])
        abuf = [w[:, n * BANK:(n + 1) * BANK] for w in (wk_sb, wv_sb) for n in range(2)]
        pacc = sb("pacc", [P, 2, BANK])
        pfold = sb("pfold", [P, 2 * D])
        psum2 = sb("psum2", [P, 2, D])
        o_sb = x_in
        y_sb = x1

        sim = ctx.enter_context(nc.psum_tensor("sim", [P, 2 * BANK], F32))
        attn_ps, misc_ps, *slot_ps = [
            ctx.enter_context(nc.psum_tensor(n, [P, BANK], F32))
            for n in ("attn_ps", "misc_ps", *(f"slot{n}_ps" for n in range(FB)))]
        maxT_ps = misc_ps[0:2 * H, 0:P]
        xnT_ps = misc_ps[:, P:2 * P]
        av_ps = misc_ps[:, 2 * P:3 * P]
        logits_ps = misc_ps[:, 3 * P:3 * P + E]

        ld = {n: sem(f"ld_{n}") for n in ("ctx", "wk0", "wk1", "wq0", "wq1", "x0", "x1", "ident", "sel",
                                          "iota", "wv", "wo", "rw", "we0", "we1", "we2", "we3")}
        out_stored = sem("out_stored")
        zeroed = sem("zeroed")
        sel_ready = sem("sel_ready")
        fill_ready = sem("fill_ready")
        fill_act = sem("fill_act")
        fill_dve = sem("fill_dve")
        stats1 = sem("stats1")
        ve1_ready = sem("ve1_ready")
        rstd1_ready = sem("rstd1_ready")
        y_ready = sem("y_ready")
        yt_ready = sem("yt_ready")
        yt_hi_ready = sem("yt_hi_ready")
        yt_lo_ready = sem("yt_lo_ready")
        we_hi_ready = sem("we_hi_ready")
        we_lo_ready = sem("we_lo_ready")
        sim_ready = sem("sim_ready")
        nmax_done = sem("nmax_done")
        nmax_hi_done = sem("nmax_hi_done")
        nmax_ready = sem("nmax_ready")
        nmaxT_ready = sem("nmaxT_ready")
        nmaxT_copied = sem("nmaxT_copied")
        shifted = sem("shifted")
        exp_done = sem("exp_done")
        sum_done = sem("sum_done")
        rsum_ready = sem("rsum_ready")
        norm_done = sem("norm_done")
        attnT_ready = sem("attnT_ready")
        attnT_copied = sem("attnT_copied")
        av_ready = sem("av_ready")
        x1_done = sem("x1_done")
        stats2 = sem("stats2")
        ve2_ready = sem("ve2_ready")
        rstd2_ready = sem("rstd2_ready")
        xn_ready = sem("xn_ready")
        xnT_ready = sem("xnT_ready")
        xt_ready = sem("xt_ready")
        xt_hi_ready = sem("xt_hi_ready")
        xt_split = sem("xt_split")
        logits_ready = sem("logits_ready")
        logits_copied = sem("logits_copied")
        top_done = sem("top_done")
        ntop_ready = sem("ntop_ready")
        idx_done = sem("idx_done")
        m1_done = sem("m1_done")
        m12_done = sem("m12_done")
        el_ready = sem("el_ready")
        er_done = sem("er_done")
        w_ready = sem("w_ready")
        ffn_ready = sem("ffn_ready")
        acc_step = sem("acc_step")
        act_weighed = sem("act_weighed")
        pool_added = sem("pool_added")
        folded = sem("folded")
        acc_merged = sem("acc_merged")
        o_ready = sem("o_ready")

        block = ctx.enter_context(nc.Block())

        def of_dve(j, c):
            return c in (DVE_CHUNKS if j < NT - 1 else LAST_DVE_CHUNKS)

        def in_dve(k):
            return sum(of_dve(n // EC, n % EC) for n in range(k))

        def in_act(k):
            return k - in_dve(k)

        def steps():
            for i in range(NT + LAG):
                yield (i, *(0 <= i - d < NT for d in (0, 1, 2, LAG)))

        @block.sync
        def _(sp):
            sp.dma_start(ctx_t[:, :, :], ctxT).then_inc(ld["ctx"], 16)
            for n in range(2):
                w = slice(n * H * DH // 2, (n + 1) * H * DH // 2)
                sp.dma_start(wk_sb[:, w], wk[:, w]).then_inc(ld[f"wk{n}"], 16)
            for n in range(2):
                w = slice(n * C // 2, (n + 1) * C // 2)
                sp.dma_start(wq_sb[:, w, :], wqT[:, w, :]).then_inc(ld[f"wq{n}"], 16)
            sp.dma_start(wv_sb[:, :], wv).then_inc(ld["wv"], 16)
            sp.dma_start(wo_sb[:, :, :], wo).then_inc(ld["wo"], 16)
            for n in range(4):
                w = slice(n * E * D // 4, (n + 1) * E * D // 4)
                sp.dma_start(we_sb[:, w], we[:, w]).then_inc(ld[f"we{n}"], 16)
            for j in range(NT):
                sp.wait_ge(o_ready, j + 1)
                sp.dma_start(out[:, j, :], o_sb[:, j, :]).then_inc(out_stored, 16)
            sp.wait_ge(out_stored, 16 * NT)

        @block.tensor
        def _(pe):
            def fill(n):
                what, b, half = FILLS[n]
                ps = slot_ps[n % FB]
                if n >= FB:
                    pe.wait_ge(fill_act, n - FB + 1)
                    pe.wait_ge(fill_dve, dve_fills(n - FB + 1))
                if what == "K" and b == 0:
                    if half == 0:
                        pe.wait_ge(ld["ctx"], 16)
                    pe.wait_ge(ld[f"wk{half}"], 16)
                if what == "G" and half == 0:
                    pe.wait_ge(fill_act, filled("K", b // 2 * 2))
                    pe.wait_ge(fill_dve, dve_fills(filled("K", b // 2 * 2)))
                if what == "G" and b == 0:
                    pe.wait_ge(ld[f"wq{half}"], 16)
                if what == "V" and b == 0 and half == 0:
                    pe.wait_ge(ld["wv"], 16)
                if what == "U" and half == 0:
                    pe.wait_ge(fill_act, filled("V", b // 2 * 2))
                    pe.wait_ge(fill_dve, dve_fills(filled("V", b // 2 * 2)))
                    if b == 0:
                        pe.wait_ge(ld["wo"], 16)
                for q in range(4):
                    c = 4 * half + q
                    if what in "KV":
                        w = wk_sb if what == "K" else wv_sb
                        lhs, rhs = w[:, c * P:(c + 1) * P], ctx_t[:, b:b + 2, :]
                    elif what == "G":
                        lhs, rhs = wq_sb[:, c, :], kt_bd[:, c, b, :]
                    else:
                        lhs, rhs = vt_bd[:, c, b, :], wo_sb[:, c, :]
                    mm = nc.tensor.matmul(ps[:, q * P:(q + 1) * P], lhs, rhs, start=True, stop=True)
                mm.then_inc(fill_ready, 1)

            def turn_y(q):
                pe.wait_ge(y_ready, 4 * (q + 1))
                if q == 0:
                    pe.wait_ge(ld["ident"], 16)
                else:
                    pe.wait_ge(yt_lo_ready, q)
                for t in range(4):
                    mm = nc.tensor.transpose(attn_ps[:, t * P:(t + 1) * P], y_sb[:, 4 * q + t, :], ident[:, :])
                mm.then_inc(yt_ready, 1)

            def scores(i):
                b = i // TB
                if i:
                    pe.wait_ge(exp_done, i)
                if i % TB == 0:
                    pe.wait_ge(fill_dve, dve_fills(filled("G", b)))
                if i % 4 == 0:
                    pe.wait_ge(yt_lo_ready, i // 4 + 1)
                for s in range(2):
                    w = slice(s * BANK, (s + 1) * BANK)
                    nc.tensor.matmul(sim[:, w], yt_hi[:, i, :], g_hi[:, b, w], start=True, stop=False)
                    nc.tensor.matmul(sim[:, w], yt_hi[:, i, :], g_lo[:, b, w], start=False, stop=False)
                    mm = nc.tensor.matmul(sim[:, w], yt_lo[:, i, :], g_hi[:, b, w], start=False, stop=True)
                mm.then_inc(sim_ready, 1)

            def turn_max(i):
                pe.wait_ge(nmax_ready, i + 1)
                if i >= 2:
                    pe.wait_ge(logits_copied, i - 1)
                nc.tensor.transpose(maxT_ps, nmax_hl[:, i % 2, :].bitcast(F32), ident[:, :]).then_inc(nmaxT_ready, 1)

            def subtract_max(i):
                pe.wait_ge(nmaxT_copied, i + 1)
                if i == 0:
                    pe.wait_ge(sel_ready, 1)
                for s in range(2):
                    w = slice(s * BANK, (s + 1) * BANK)
                    mm = nc.tensor.matmul(sim[:, w], nmaxT[:, i % 2, :], sel[:, w], start=False, stop=True,
                                          skip_group_check=True)
                mm.then_inc(shifted, 1)

            def turn_attn(i, half):
                if half == 0:
                    pe.wait_ge(norm_done, i + 1)
                if i == 0 and half == 0:
                    pe.wait_ge(yt_lo_ready, 2)
                if 2 * i + half >= 1:
                    pe.wait_ge(attnT_copied, 2 * i + half)
                for q in range(4):
                    c = 4 * half + q
                    mm = nc.tensor.transpose(attn_ps[:, q * P:(q + 1) * P],
                                             prob[:, i % 2, 2 * c:2 * c + 2, :], ident[:, :])
                mm.then_inc(attnT_ready, 1)

            def attend(i):
                pe.wait_ge(attnT_copied, 2 * i + 2)
                if i:
                    pe.wait_ge(x1_done, i)
                if i % TB == 0:
                    pe.wait_ge(fill_act, filled("U", i // TB))
                for c in range(C):
                    mm = nc.tensor.matmul(av_ps, at[:, i % 2, c, :], u_sb[:, i // TB, c, :],
                                          start=(c == 0), stop=(c == C - 1))
                mm.then_inc(av_ready, 1)

            def turn_xn(i):
                pe.wait_ge(xn_ready, i + 1)
                if i + 1 < NT:
                    pe.wait_ge(nmaxT_copied, i + 2)
                if i:
                    pe.wait_ge(logits_copied, i)
                nc.tensor.transpose(xnT_ps, xn[:, i % 2, :], ident[:, :]).then_inc(xnT_ready, 1)

            def router(i):
                pe.wait_ge(xt_hi_ready, i + 1)
                if i == 0:
                    pe.wait_ge(ld["rw"], 16)
                nc.tensor.matmul(logits_ps, xt[:, i % 2, :], rw_sb[:, :], start=True, stop=True).then_inc(logits_ready, 1)

            def slot(i, c):
                if i < LAG:
                    return fill(EC * i + c)
                j = i - LAG
                if j >= NT:
                    return
                k = EC * j + c
                if c == 0:
                    pe.wait_ge(xt_split, j + 1)
                if k < EC and k % 2 == 0:
                    pe.wait_ge(we_lo_ready, k // 2 + 1)
                if k < FB:
                    n = len(FILLS) - FB + k + 1
                    pe.wait_ge(fill_act, n)
                    pe.wait_ge(fill_dve, dve_fills(n))
                elif of_dve((k - FB) // EC, (k - FB) % EC):
                    pe.wait_ge(acc_step, EB * in_dve(k - FB + 1))
                else:
                    pe.wait_ge(act_weighed, in_act(k - FB + 1))
                o = slot_ps[k % FB][:, :]
                w = slice(c * BANK, (c + 1) * BANK)
                nc.tensor.matmul(o, xt_hi[:, j % 2, :], we_hi[:, w], start=True, stop=False)
                nc.tensor.matmul(o, xt_hi[:, j % 2, :], we_lo[:, w], start=False, stop=False)
                nc.tensor.matmul(o, xt_lo[:, j % 2, :], we_hi[:, w], start=False,
                                 stop=True).then_inc(ffn_ready, 1)

            for i, tile0, tile1, tile2, experts in steps():
                if i == 0:
                    slot(0, 0)
                    slot(0, 1)
                    turn_y(0)
                    slot(0, 2)
                    slot(0, 3)
                    slot(0, 4)
                    slot(0, 5)
                    scores(0)
                    slot(0, 6)
                    slot(0, 7)
                    turn_max(0)
                    turn_y(1)
                    subtract_max(0)
                    continue
                if i < LAG:
                    slot(i, 0)
                    slot(i, 1)
                    scores(i)
                    if tile2:
                        turn_xn(i - 2)
                    slot(i, 2)
                    slot(i, 3)
                    turn_attn(i - 1, 0)
                    if tile2:
                        router(i - 2)
                    turn_max(i)
                    slot(i, 4)
                    turn_attn(i - 1, 1)
                    subtract_max(i)
                    attend(i - 1)
                    slot(i, 5)
                    slot(i, 6)
                    slot(i, 7)
                    continue
                slot(i, 0)
                if tile0:
                    scores(i)
                if tile2:
                    turn_xn(i - 2)
                slot(i, 1)
                if tile1:
                    turn_attn(i - 1, 0)
                if tile2:
                    router(i - 2)
                slot(i, 2)
                if tile1:
                    turn_attn(i - 1, 1)
                if tile0:
                    turn_max(i)
                slot(i, 3)
                slot(i, 4)
                if tile0:
                    subtract_max(i)
                if tile1:
                    attend(i - 1)
                slot(i, 5)
                slot(i, 6)
                slot(i, 7)

        @block.vector
        def _(dve):
            def layer_norm_1(q):
                dve.wait_ge(ld[f"x{q}"], 16)
                for t in range(4 * q, 4 * q + 4):
                    nc.vector.bn_stats(st1[:, t, :], x_in[:, t, :]).then_inc(stats1, 1)
                for t in range(4 * q, 4 * q + 4):
                    dve.wait_ge(stats1, 4 * q + t + 1)
                    nc.vector.bn_aggr(mv1[:, t, :], st1[:, t, :]).then_inc(stats1, 1)
                dve.wait_ge(stats1, 8 * q + 8)
                nc.vector.tensor_scalar(ve1[:, 4 * q:4 * q + 4], mv1[:, 4 * q:4 * q + 4, 1], EPS, None,
                                        ALU.add).then_inc(ve1_ready, 1)

            def apply_norm_1(q):
                dve.wait_ge(rstd1_ready, q + 1)
                for t in range(4 * q, 4 * q + 4):
                    nc.vector.tensor_scalar(y_sb[:, t, :], x_in[:, t, :], mv1[:, t, 0:1], rstd1[:, t:t + 1],
                                            ALU.subtract, ALU.mult).then_inc(y_ready, 1)

            def rest_y(q):
                dve.wait_ge(yt_hi_ready, q + 1)
                nc.vector.tensor_tensor(yt_lo[:, 4 * q:4 * q + 4, :],
                                        attn_ps[:, :].rearrange("p (t n) -> p t n", t=4),
                                        yt_hi[:, 4 * q:4 * q + 4, :].bitcast(F32),
                                        ALU.subtract).then_inc(yt_lo_ready, 1)

            def max_of(i):
                dve.wait_ge(sim_ready, i + 1)
                nc.vector.tensor_reduce(nmax[:, i % 2, :], sim[:, :].rearrange("p (h k) -> p h k", h=H),
                                        AX.X, ALU.max, negate=True).then_inc(nmax_done, 1)

            def max_hi(i):
                dve.wait_ge(nmax_done, i + 1)
                if i >= 2:
                    dve.wait_ge(nmaxT_ready, i - 1)
                nc.vector.tensor_copy(nmax_hl[:, i % 2, 0:H], nmax[:, i % 2, :]).then_inc(nmax_hi_done, 1)

            def max_lo(i):
                dve.wait_ge(nmax_hi_done, i + 1)
                nc.vector.tensor_tensor(nmax_hl[:, i % 2, H:2 * H], nmax[:, i % 2, :],
                                        nmax_hl[:, i % 2, 0:H].bitcast(F32), ALU.subtract).then_inc(nmax_ready, 1)

            def sum_of(i):
                dve.wait_ge(exp_done, i + 1)
                nc.vector.tensor_reduce(psum_h[:, i % 2, :], prob[:, i % 2, :, :], AX.X, ALU.add).then_inc(sum_done, 1)

            def sum_inverse(i):
                dve.wait_ge(sum_done, i + 1)
                if i >= 2:
                    dve.wait_ge(norm_done, i - 1)
                nc.vector.reciprocal(rsum_h[:, i % 2, :], psum_h[:, i % 2, :]).then_inc(rsum_ready, 1)

            def residual(i):
                dve.wait_ge(av_ready, i + 1)
                nc.vector.tensor_tensor(x1[:, i, :], av_ps, x_in[:, i, :], ALU.add).then_inc(x1_done, 1)

            def stats_2(i):
                dve.wait_ge(x1_done, i + 1)
                nc.vector.bn_stats(st2[:, i, :], x1[:, i, :]).then_inc(stats2, 1)

            def aggregate_2(i):
                dve.wait_ge(stats2, 2 * i + 1)
                nc.vector.bn_aggr(mv2[:, i, :], st2[:, i, :]).then_inc(stats2, 1)

            def variance_2(i):
                dve.wait_ge(stats2, 2 * i + 2)
                nc.vector.tensor_scalar(ve2[:, i:i + 1], mv2[:, i, 1:2], EPS, None, ALU.add).then_inc(ve2_ready, 1)

            def apply_norm_2(i):
                dve.wait_ge(rstd2_ready, i + 1)
                if i >= 2:
                    dve.wait_ge(xnT_ready, i - 1)
                nc.vector.tensor_scalar(xn[:, i % 2, :], x1[:, i, :], mv2[:, i, 0:1], rstd2[:, i:i + 1],
                                        ALU.subtract, ALU.mult).then_inc(xn_ready, 1)

            def rest_xt(i):
                dve.wait_ge(xt_hi_ready, i + 1)
                if i >= 2:
                    dve.wait_ge(ffn_ready, EC * (i - 1))
                nc.vector.tensor_tensor(xt_lo[:, i % 2, :], xt[:, i % 2, :], xt_hi[:, i % 2, :].bitcast(F32),
                                        ALU.subtract).then_inc(xt_split, 1)

            def top_values(i):
                dve.wait_ge(logits_copied, i + 1)
                nc.vector.max(top8[:, i % 2, :], lg[:, i % 2, :]).then_inc(top_done, 1)

            def minus_top(i):
                dve.wait_ge(top_done, i + 1)
                nc.vector.tensor_scalar(ntop[:, i % 2, :], top8[:, i % 2, 0:1], -1.0, None, ALU.mult).then_inc(ntop_ready, 1)

            def top_places(i):
                nc.vector.max_index(idx8[:, i % 2, :], top8[:, i % 2, :], lg[:, i % 2, :]).then_inc(idx_done, 1)

            def mask_first(i):
                dve.wait_ge(idx_done, i + 1)
                nc.vector.tensor_scalar(m1[:, i % 2, :], iota[:, :], idx8[:, i % 2, 0:1], None,
                                        ALU.is_equal).then_inc(m1_done, 1)

            def mask_both(i):
                dve.wait_ge(m1_done, i + 1)
                nc.vector.scalar_tensor_tensor(m12[:, i % 2, :], iota[:, :], idx8[:, i % 2, 1:2], m1[:, i % 2, :],
                                               ALU.is_equal, ALU.add).then_inc(m12_done, 1)

            def weight_scale(i):
                dve.wait_ge(el_ready, i + 1)
                nc.vector.reciprocal(er[:, i % 2, :], es[:, i % 2, :]).then_inc(er_done, 1)

            def weights(i):
                p = i % 2
                dve.wait_ge(er_done, i + 1)
                dve.wait_ge(m12_done, i + 1)
                if i >= 2:
                    dve.wait_ge(act_weighed, NA * (i - 1))
                nc.vector.scalar_tensor_tensor(wt[:, p, :], el[:, p, :], er[:, p, 0:1], m12[:, p, :],
                                               ALU.mult, ALU.mult).then_inc(w_ready, 1)

            def slot(i, c, *quarters):
                if i < LAG:
                    if 0 in quarters:
                        fill(EC * i + c)
                    return
                j = i - LAG
                if j >= NT or not of_dve(j, c):
                    return
                k = EC * j + c
                for q in quarters:
                    n = EB * in_dve(k) + q
                    first = n - EB * in_dve(EC * j)
                    if q == 0:
                        dve.wait_ge(ffn_ready, k + 1)
                    if first == 0:
                        dve.wait_ge(w_ready, j + 1)
                        if j >= 2:
                            dve.wait_ge(acc_merged, j - 1)
                    if first >= 2:
                        dve.wait_ge(acc_step, n - 1)
                    y = slot_ps[k % FB][:, q * D:(q + 1) * D]
                    w = wt[:, j % 2, EB * c + q:EB * c + q + 1]
                    if first == 1:
                        ins = nc.vector.tensor_scalar(acc[:, j % 2, 1, :], y, w, None, ALU.mult)
                    else:
                        chain = acc[:, j % 2, n % 2, :]
                        before = x1[:, j, :] if first == 0 else chain
                        ins = nc.vector.scalar_tensor_tensor(chain, y, w, before, ALU.mult, ALU.add)
                    ins.then_inc(acc_step, 1)

            def merge(j):
                steps_done = EB * in_dve(EC * (j + 1))
                dve.wait_ge(folded, 2 * j + 2)
                dve.wait_ge(acc_step, steps_done - 1)
                nc.vector.tensor_tensor(psum2[:, 1, :], psum2[:, 0, :], acc[:, j % 2, 0, :],
                                        ALU.add).then_inc(acc_merged, 1)
                dve.wait_ge(acc_merged, j + 1)
                dve.wait_ge(acc_step, steps_done)
                nc.vector.tensor_tensor(o_sb[:, j, :], psum2[:, 1, :], acc[:, j % 2, 1, :],
                                        ALU.add).then_inc(o_ready, 1)

            def fill(n):
                what, b, half = FILLS[n]
                ps = slot_ps[n % FB]
                c = slice(4 * half, 4 * half + 4)
                if what in "KV":
                    dst = kt_bd if what == "K" else vt_bd
                    dve.wait_ge(fill_ready, n + 1)
                    nc.vector.tensor_copy(dst[M:P, c, b:b + 2, M:2 * M],
                                          ps[M:P, :].rearrange("p (c b k) -> p c b k", c=4, b=2)
                                          ).then_inc(fill_dve, 1)
                if what == "G":
                    w = slice(half * BANK, (half + 1) * BANK)
                    dve.wait_ge(fill_act, n + 1)
                    nc.vector.tensor_tensor(g_lo[:, b, w], ps[:, :], g_hi[:, b, w].bitcast(F32),
                                            ALU.subtract).then_inc(fill_dve, 1)

            def round_experts(n):
                dve.wait_ge(ld[f"we{n}"], 16)
                w = slice(n * E * D // 4, (n + 1) * E * D // 4)
                nc.vector.tensor_copy(we_hi[:, w], we_sb[:, w]).then_inc(we_hi_ready, 1)

            for i, tile0, tile1, tile2, experts in steps():
                if i == 0:
                    nc.vector.memset(vt_bd[M:P, :, :, 0:M], 0.0)
                    layer_norm_1(0)
                    slot(0, 0, 0)
                    apply_norm_1(0)
                    slot(0, 1, 0)
                    layer_norm_1(1)
                    rest_y(0)
                    slot(0, 2, 0)
                    slot(0, 3, 0)
                    slot(0, 4, 0)
                    slot(0, 5, 0)
                    apply_norm_1(1)
                    max_of(0)
                    max_hi(0)
                    max_lo(0)
                    dve.wait_ge(ld["sel"], 16)
                    nc.vector.tensor_copy(sel[:, :], sel_in[:, :]).then_inc(sel_ready, 1)
                    dve.wait_ge(ld["iota"], 16)
                    round_experts(0)
                    rest_y(1)
                    sum_of(0)
                    sum_inverse(0)
                    continue
                if i < LAG:
                    slot(i, 0, 0)
                    slot(i, 1, 0)
                    max_of(i)
                    max_hi(i)
                    max_lo(i)
                    slot(i, 2, 0)
                    if tile2:
                        rest_xt(i - 2)
                    slot(i, 3, 0)
                    if tile2:
                        top_values(i - 2)
                        minus_top(i - 2)
                        top_places(i - 2)
                        mask_first(i - 2)
                        mask_both(i - 2)
                    slot(i, 4, 0)
                    sum_of(i)
                    residual(i - 1)
                    sum_inverse(i)
                    stats_2(i - 1)
                    slot(i, 5, 0)
                    aggregate_2(i - 1)
                    variance_2(i - 1)
                    if tile2:
                        weight_scale(i - 2)
                        weights(i - 2)
                    round_experts(i)
                    apply_norm_2(i - 1)
                    if i == LAG - 1:
                        round_experts(LAG)
                    continue
                slot(i, 0, 0, 1, 2, 3)
                if tile0:
                    max_of(i)
                slot(i, 1, 0)
                if tile0:
                    max_hi(i)
                slot(i, 1, 1)
                if tile0:
                    max_lo(i)
                if tile2:
                    rest_xt(i - 2)
                slot(i, 1, 2)
                if tile2:
                    top_values(i - 2)
                if tile2:
                    minus_top(i - 2)
                    top_places(i - 2)
                slot(i, 1, 3)
                slot(i, 2, 0, 1, 2, 3)
                if tile2:
                    mask_first(i - 2)
                slot(i, 3, 0)
                if tile2:
                    mask_both(i - 2)
                slot(i, 3, 1, 2, 3)
                if NT - DVE_MERGED < i - LAG < NT:
                    merge(i - LAG - 1)
                if tile0:
                    sum_of(i)
                if tile1:
                    residual(i - 1)
                if tile0:
                    sum_inverse(i)
                if tile1:
                    stats_2(i - 1)
                slot(i, 4, 0, 1, 2, 3)
                slot(i, 5, 0)
                if tile1:
                    aggregate_2(i - 1)
                slot(i, 5, 1)
                if tile1:
                    variance_2(i - 1)
                slot(i, 5, 2)
                if tile2:
                    weight_scale(i - 2)
                slot(i, 5, 3)
                if tile2:
                    weights(i - 2)
                slot(i, 6, 0, 1, 2, 3)
                if tile1:
                    apply_norm_2(i - 1)
                slot(i, 7, 0, 1, 2, 3)
                if i - LAG == NT - 1:
                    merge(NT - 1)

        @block.scalar
        def _(act):
            act.dma_start(x_in[:, 0:4, :], x[:, 0:4, :]).then_inc(ld["x0"], 16)
            act.dma_start(ident[:, :], ident_d).then_inc(ld["ident"], 16)
            act.dma_start(x_in[:, 4:8, :], x[:, 4:8, :]).then_inc(ld["x1"], 16)
            act.dma_start(sel_in[:, :], sel_d).then_inc(ld["sel"], 16)
            act.dma_start(iota[:, :], iota_d).then_inc(ld["iota"], 16)
            act.dma_start(rw_sb[:, :], rwT).then_inc(ld["rw"], 16)

            def round_y(q):
                act.wait_ge(yt_ready, q + 1)
                nc.scalar.activation(yt_hi[:, 4 * q:4 * q + 4, :],
                                     attn_ps[:, :].rearrange("p (t n) -> p t n", t=4),
                                     ACT.Copy).then_inc(yt_hi_ready, 1)

            def copy_maxT(i):
                act.wait_ge(nmaxT_ready, i + 1)
                if i >= 2:
                    act.wait_ge(shifted, i - 1)
                nc.scalar.activation(nmaxT[:, i % 2, :], maxT_ps, ACT.Copy).then_inc(nmaxT_copied, 1)

            def exponentials(i):
                act.wait_ge(shifted, i + 1)
                if i >= 2:
                    act.wait_ge(attnT_ready, 2 * (i - 1))
                nc.scalar.activation(prob[:, i % 2, :, :], sim[:, :].rearrange("p (h k) -> p h k", h=H),
                                     ACT.Exp, scale=SCALE).then_inc(exp_done, 1)

            def copy_attnT(i, half):
                act.wait_ge(attnT_ready, 2 * i + half + 1)
                if i >= 2:
                    act.wait_ge(av_ready, i - 1)
                nc.scalar.activation(at[:, i % 2, 4 * half:4 * half + 4, :],
                                     attn_ps[:, :].rearrange("p (c n) -> p c n", c=4),
                                     ACT.Copy).then_inc(attnT_copied, 1)

            def copy_xnT(i):
                act.wait_ge(xnT_ready, i + 1)
                if i >= 2:
                    act.wait_ge(xt_split, i - 1)
                    act.wait_ge(logits_ready, i - 1)
                    act.wait_ge(ffn_ready, EC * (i - 1))
                nc.scalar.activation(xt[:, i % 2, :], xnT_ps, ACT.Copy).then_inc(xt_ready, 1)
                nc.scalar.activation(xt_hi[:, i % 2, :], xnT_ps, ACT.Copy).then_inc(xt_hi_ready, 1)

            def copy_logits(i):
                act.wait_ge(logits_ready, i + 1)
                if i >= 2:
                    act.wait_ge(idx_done, i - 1)
                nc.scalar.activation(lg[:, i % 2, :], logits_ps, ACT.Copy).then_inc(logits_copied, 1)

            def router_exp(i):
                act.wait_ge(ntop_ready, i + 1)
                act.wait_ge(logits_copied, i + 1)
                if i >= 2:
                    act.wait_ge(w_ready, i - 1)
                nc.scalar.activation(el[:, i % 2, :], lg[:, i % 2, :], ACT.Exp, bias=ntop[:, i % 2, 0:1],
                                     accum_out=es[:, i % 2, 0:1]).then_inc(el_ready, 1)

            def slot(i, c):
                if i < LAG:
                    return fill(EC * i + c)
                j = i - LAG
                if j >= NT or of_dve(j, c):
                    return
                k = EC * j + c
                n = in_act(k)
                act.wait_ge(ffn_ready, k + 1)
                act.wait_ge(w_ready, j + 1)
                if n >= len(abuf):
                    before = n - len(abuf)
                    act.wait_ge(pool_added, (NA - 1) * (before // NA) + max(before % NA, 1))
                for q in range(EB):
                    e = EB * c + q
                    ins = nc.scalar.activation(abuf[n % len(abuf)][:, q * D:(q + 1) * D],
                                               slot_ps[k % FB][:, q * D:(q + 1) * D], ACT.Copy,
                                               scale=wt[:, j % 2, e:e + 1])
                ins.then_inc(act_weighed, 1)

            def fill(n):
                what, b, half = FILLS[n]
                ps = slot_ps[n % FB]
                c = slice(4 * half, 4 * half + 4)
                w = slice(half * BANK, (half + 1) * BANK)
                if n == 0:
                    act.wait_ge(zeroed, 3)
                if what == "V" and n == FILLS.index(("V", 0, 0)):
                    act.wait_ge(zeroed, 4)
                act.wait_ge(fill_ready, n + 1)
                if what in "KV":
                    dst = kt_bd if what == "K" else vt_bd
                    ins = nc.scalar.activation(dst[0:M, c, b:b + 2, 0:M],
                                               ps[0:M, :].rearrange("p (c b k) -> p c b k", c=4, b=2), ACT.Copy)
                elif what == "G":
                    ins = nc.scalar.activation(g_hi[:, b, w], ps[:, :], ACT.Copy)
                else:
                    ins = nc.scalar.activation(u_sb[:, b, c, :], ps[:, :].rearrange("p (c d) -> p c d", c=4), ACT.Copy)
                ins.then_inc(fill_act, 1)

            act.wait_ge(zeroed, 1)
            nc.scalar.activation(warm[:, :], mhalf[:, 0:1], ACT.Exp)
            for i, tile0, tile1, tile2, experts in steps():
                if i == 0:
                    slot(0, 0)
                    slot(0, 1)
                    round_y(0)
                    slot(0, 2)
                    slot(0, 3)
                    slot(0, 4)
                    slot(0, 5)
                    slot(0, 6)
                    slot(0, 7)
                    copy_maxT(0)
                    round_y(1)
                    exponentials(0)
                    continue
                if i < LAG:
                    slot(i, 0)
                    slot(i, 1)
                    if tile2:
                        copy_xnT(i - 2)
                    slot(i, 2)
                    slot(i, 3)
                    copy_attnT(i - 1, 0)
                    if tile2:
                        copy_logits(i - 2)
                    copy_maxT(i)
                    slot(i, 4)
                    copy_attnT(i - 1, 1)
                    exponentials(i)
                    if tile2:
                        router_exp(i - 2)
                    slot(i, 5)
                    slot(i, 6)
                    slot(i, 7)
                    continue
                if tile2:
                    copy_xnT(i - 2)
                slot(i, 1)
                if tile1:
                    copy_attnT(i - 1, 0)
                if tile2:
                    copy_logits(i - 2)
                slot(i, 0)
                if tile1:
                    copy_attnT(i - 1, 1)
                if tile0:
                    copy_maxT(i)
                slot(i, 2)
                slot(i, 3)
                if tile0:
                    exponentials(i)
                if tile2:
                    router_exp(i - 2)
                slot(i, 4)
                slot(i, 5)
                slot(i, 6)
                slot(i, 7)

        @block.gpsimd
        def _(pool):
            nc.gpsimd.memset(mhalf[:, :], -0.5).then_inc(zeroed, 1)
            pool.wait_ge(zeroed, 1)
            nc.gpsimd.memset(kt_bd[0:M, :, :, M:2 * M], 0.0).then_inc(zeroed, 1)
            pool.wait_ge(zeroed, 2)
            nc.gpsimd.memset(kt_bd[M:P, :, :, 0:M], 0.0).then_inc(zeroed, 1)
            pool.wait_ge(zeroed, 3)

            def rstd_1(q):
                pool.wait_ge(ve1_ready, q + 1)
                nc.gpsimd.tensor_tensor(rstd1[:, 4 * q:4 * q + 4], ve1[:, 4 * q:4 * q + 4], mhalf[:, 0:4],
                                        ALU.pow).then_inc(rstd1_ready, 1)

            def rest_experts(n):
                pool.wait_ge(we_hi_ready, n + 1)
                w = slice(n * E * D // 4, (n + 1) * E * D // 4)
                nc.gpsimd.tensor_tensor(we_lo[:, w], we_sb[:, w], we_hi[:, w].bitcast(F32),
                                        ALU.subtract).then_inc(we_lo_ready, 1)

            def normalise_probs(i):
                pool.wait_ge(rsum_ready, i + 1)
                nc.gpsimd.tensor_tensor(prob[:, i % 2, :, :], prob[:, i % 2, :, :],
                                        rsum_h[:, i % 2, :].unsqueeze(2).broadcast_to([P, H, M]),
                                        ALU.mult).then_inc(norm_done, 1)

            def rstd_2(i):
                pool.wait_ge(ve2_ready, i + 1)
                nc.gpsimd.tensor_tensor(rstd2[:, i:i + 1], ve2[:, i:i + 1], mhalf[:, 0:1],
                                        ALU.pow).then_inc(rstd2_ready, 1)

            def slot(i, c):
                j = i - LAG
                if not 0 <= j < NT or of_dve(j, c):
                    return
                n = in_act(EC * j + c)
                m = n - NA * j
                if m == 0:
                    return
                pool.wait_ge(act_weighed, n + 1)
                if m == 1:
                    before = abuf[(n - 1) % len(abuf)]
                else:
                    pool.wait_ge(pool_added, (NA - 1) * j + m - 1)
                    before = pacc[:, m % 2, :]
                nc.gpsimd.tensor_tensor(pacc[:, (m + 1) % 2, :], before, abuf[n % len(abuf)],
                                        ALU.add).then_inc(pool_added, 1)

            def fold(j):
                banks = in_act(EC * (j + 1)) - NA * j
                pool.wait_ge(pool_added, (NA - 1) * j + banks - 1)
                a = pacc[:, banks % 2, :]
                nc.gpsimd.tensor_tensor(pfold[:, :], a[:, 0:2 * D], a[:, 2 * D:4 * D], ALU.add).then_inc(folded, 1)
                pool.wait_ge(folded, 2 * j + 1)
                if j > NT - DVE_MERGED:
                    pool.wait_ge(acc_merged, j)
                nc.gpsimd.tensor_tensor(psum2[:, 0, :], pfold[:, 0:D], pfold[:, D:2 * D], ALU.add).then_inc(folded, 1)

            def merge(j):
                pool.wait_ge(acc_step, EB * ND * (j + 1))
                nc.gpsimd.tensor_tensor(psum2[:, 1, :], acc[:, j % 2, 0, :], acc[:, j % 2, 1, :], ALU.add).then_inc(acc_merged, 1)
                pool.wait_ge(acc_merged, j + 1)
                pool.wait_ge(folded, 2 * j + 2)
                nc.gpsimd.tensor_tensor(o_sb[:, j, :], psum2[:, 0, :], psum2[:, 1, :], ALU.add).then_inc(o_ready, 1)

            rstd_1(0)
            rstd_1(1)
            nc.gpsimd.memset(vt_bd[0:M, :, :, M:2 * M], 0.0).then_inc(zeroed, 1)
            pool.wait_ge(zeroed, 4)
            for i, tile0, tile1, tile2, experts in steps():
                slot(i, 0)
                slot(i, 1)
                slot(i, 2)
                slot(i, 3)
                if tile1:
                    rstd_2(i - 1)
                if tile0:
                    normalise_probs(i)
                if i < LAG:
                    rest_experts(i)
                slot(i, 4)
                slot(i, 5)
                slot(i, 6)
                slot(i, 7)
                if i == LAG - 1:
                    rest_experts(LAG)
                if experts:
                    fold(i - LAG)
                    if i - LAG < NT - DVE_MERGED:
                        merge(i - LAG)


_OUT = (B, N, D)


def kernel(**inputs):
    import concourse.bacc as _bacc
    from concourse.bass_utils import run_bass_kernel_spmd as _run

    a = {k: np.asarray(v) for k, v in inputs.items()}
    laid = {
        "x": a["x"].reshape(NT, P, D).transpose(1, 0, 2),
        "ctxT": a["ctx_1024"].transpose(2, 0, 1),
        "wk": a["L0_xattn_Wk"],
        "wqT": a["L0_xattn_Wq"].T.reshape(C, P, D).transpose(1, 0, 2),
        "wv": a["L0_xattn_Wv"],
        "wo": a["L0_xattn_Wo"].reshape(C, P, D).transpose(1, 0, 2),
        "rwT": a["L0_ffn_router_w"].T,
        "we": a["L0_ffn_expert_weights"].transpose(1, 0, 2).reshape(D, E * D),
        "ident": np.eye(P, dtype=np.float32),
        "sel": np.tile(np.repeat(np.eye(H, dtype=np.float32), M, axis=1), (2, 1)),
        "iota": np.tile(np.arange(E, dtype=np.float32), (P, 1)),
    }
    nc = _bacc.Bacc("TRN2", target_bir_lowering=False, num_devices=1)
    arrays, args = {}, []
    for name, v in laid.items():
        v = np.ascontiguousarray(v)
        arrays[f"in_{name}"] = v
        args.append(nc.dram_tensor(f"in_{name}", v.shape, mybir.dt.from_np(v.dtype), kind="ExternalInput").ap())
    args.append(nc.dram_tensor("out_0", (P, NT, D), F32, kind="ExternalOutput").ap())
    build(nc, *args)
    r = _run(nc, [arrays], core_ids=[0])
    got = r.results[0]["out_0"]
    return got.transpose(1, 0, 2).reshape(_OUT)
```

```python
from contextlib import ExitStack

import numpy as np

import concourse.bass as bass
from concourse import mybir

F32 = mybir.dt.float32
F32R = mybir.dt.float32r
U32 = mybir.dt.uint32
ALU = mybir.AluOpType
ACT = mybir.ActivationFunctionType
AX = mybir.AxisListType

P = 128
B, N, D = 4, 256, 128
M = 64
H, DH = 16, 64
E = 32
NT = B * N // P
TB = N // P
C = H * DH // P
BANK = 512
EB = BANK // D
EC = E // EB
EPS = 1e-5
WARM_UP = 8
SCALE = DH ** -0.5
DVE_CHUNKS = (1, 3, 5, 7)
ND, NA = len(DVE_CHUNKS), EC - len(DVE_CHUNKS)
DVE_MERGED = 3
SUMMED_BY_PE = 2
FB = 4
LAG = 3

FILLS = [(what, b, half) for what, b in (("K", 0), ("G", 0), ("V", 0), ("U", 0),
                                         ("K", 2), ("G", 1), ("V", 2), ("U", 1),
                                         ("G", 2), ("U", 2), ("G", 3), ("U", 3)) for half in range(2)]
assert len(FILLS) == LAG * EC and len(FILLS) % FB == 0


def dve_fills(n):
    return sum(what != "U" for what, _, _ in FILLS[:n])


def filled(what, b):
    return FILLS.index((what, b, 1)) + 1


def build(nc, x, xT, ctxT, wk, wqT, wv, wo, rwT, we, ident_d, sel_d, iota_d, out):
    with ExitStack() as ctx:
        def sb(name, shape, dt=F32):
            return ctx.enter_context(nc.sbuf_tensor(name, shape, dt))

        def sem(name):
            return ctx.enter_context(nc.semaphore(name))

        x_in = sb("x_in", [P, NT, D])
        ctx_t = sb("ctx_t", [P, B, M])
        wk_sb = sb("wk_sb", [P, H * DH])
        wq_sb = sb("wq_sb", [P, C, P])
        wv_sb = sb("wv_sb", [P, H * DH])
        wo_sb = sb("wo_sb", [P, C, D])
        rw_sb = sb("rw_sb", [P, E])
        we_sb = sb("we_sb", [P, E * D])
        we_hi = sb("we_hi", [P, E * D], F32R)
        we_lo = sb("we_lo", [P, E * D], F32R)
        ident = sb("ident", [P, P])
        sel_in = sb("sel_in", [2 * H, H * M])
        sel = sb("sel", [2 * H, H * M], F32R)
        iota = sb("iota", [P, E])
        warm = sb("warm", [P, 1])
        zeros = sb("zeros", [P, P])
        kt_bd = sb("kt_bd", [P, C, B, 2 * M])
        vt_bd = sb("vt_bd", [P, C, B, 2 * M])
        g_hi = sb("g_hi", [P, B, H * M], F32R)
        g_lo = sb("g_lo", [P, B, H * M], F32R)
        u_sb = sb("u_sb", [P, B, C, D])
        wq_sum = sb("wq_sum", [P, C])
        wq_mean = sb("wq_mean", [P, C])
        xin_hi = sb("xin_hi", [P, NT, P], F32R)
        xin_lo = sb("xin_lo", [P, NT, P], F32R)
        mhalf = sb("mhalf", [P, NT])
        st1 = sb("st1", [P, NT, 6])
        mv1 = sb("mv1", [P, NT, 2])
        ve1 = sb("ve1", [P, NT])
        rstd1 = sb("rstd1", [P, NT])
        nmax = sb("nmax", [P, 2, H])
        nmax_hl = sb("nmax_hl", [P, 2, 2 * H], F32R)
        nmaxT = sb("nmaxT", [2 * H, 2, P], F32R)
        prob = sb("prob", [P, 2, H, M])
        psum_h = sb("psum_h", [P, 2, H])
        rsum_h = sb("rsum_h", [P, 2, H])
        at = sb("at", [P, 2, C, P])
        x1 = sb("x1", [P, NT, D])
        st2 = sb("st2", [P, NT, 6])
        mv2 = sb("mv2", [P, NT, 2])
        ve2 = sb("ve2", [P, NT])
        rstd2 = sb("rstd2", [P, NT])
        xn = sb("xn", [P, 2, D])
        xt = sb("xt", [P, 2, P])
        xt_hi = sb("xt_hi", [P, 2, P], F32R)
        xt_lo = sb("xt_lo", [P, 2, P], F32R)
        lg = sb("lg", [P, 2, E])
        top8 = sb("top8", [P, 2, 8])
        ntop = sb("ntop", [P, 2, 1])
        idx8 = sb("idx8", [P, 2, 8], U32)
        m1 = sb("m1", [P, 2, E])
        m12 = sb("m12", [P, 2, E])
        el = sb("el", [P, 2, E])
        es = sb("es", [P, 2, 1])
        er = sb("er", [P, 2, 1])
        wt = sb("wt", [P, 2, E])
        acc = sb("acc", [P, 2, 2, D])
        abuf = [w[:, n * BANK:(n + 1) * BANK] for w in (wk_sb, wv_sb) for n in range(2)]
        pacc = sb("pacc", [P, 2, BANK])
        pfold = sb("pfold", [P, 2 * D])
        psum2 = sb("psum2", [P, 2, D])
        o_sb = x_in
        xin_t = x1

        sim = ctx.enter_context(nc.psum_tensor("sim", [P, 2 * BANK], F32))
        attn_ps, misc_ps, *slot_ps = [
            ctx.enter_context(nc.psum_tensor(n, [P, BANK], F32))
            for n in ("attn_ps", "misc_ps", *(f"slot{n}_ps" for n in range(FB)))]
        maxT_ps = misc_ps[0:2 * H, 0:P]
        xnT_ps = misc_ps[:, P:2 * P]
        av_ps = misc_ps[:, 2 * P:3 * P]
        logits_ps = misc_ps[:, 3 * P:3 * P + E]

        ld = {n: sem(f"ld_{n}") for n in ("ctx", "wk0", "wk1", "wq0", "wq1", "x0", "x1", "xT0", "xT1", "ident", "sel",
                                          "iota", "wv", "wo", "rw", "we0", "we1", "we2", "we3")}
        out_stored = sem("out_stored")
        zeroed = sem("zeroed")
        zeros_ready = sem("zeros_ready")
        sel_ready = sem("sel_ready")
        fill_ready = sem("fill_ready")
        fill_act = sem("fill_act")
        fill_dve = sem("fill_dve")
        stats1 = sem("stats1")
        ve1_ready = sem("ve1_ready")
        rstd1_ready = sem("rstd1_ready")
        wq_summed = sem("wq_summed")
        wq_mean_done = sem("wq_mean_done")
        wq_ready = [sem("wq0_ready"), sem("wq1_ready")]
        xin_hi_ready = sem("xin_hi_ready")
        xin_lo_ready = sem("xin_lo_ready")
        we_hi_ready = sem("we_hi_ready")
        we_lo_ready = sem("we_lo_ready")
        sim_ready = sem("sim_ready")
        nmax_done = sem("nmax_done")
        nmax_hi_done = sem("nmax_hi_done")
        nmax_ready = sem("nmax_ready")
        nmaxT_ready = sem("nmaxT_ready")
        nmaxT_copied = sem("nmaxT_copied")
        shifted = sem("shifted")
        exp_done = sem("exp_done")
        sum_done = sem("sum_done")
        rsum_ready = sem("rsum_ready")
        norm_done = sem("norm_done")
        attnT_ready = sem("attnT_ready")
        attnT_copied = sem("attnT_copied")
        av_ready = sem("av_ready")
        x1_done = sem("x1_done")
        stats2 = sem("stats2")
        ve2_ready = sem("ve2_ready")
        rstd2_ready = sem("rstd2_ready")
        xn_ready = sem("xn_ready")
        xnT_ready = sem("xnT_ready")
        xt_ready = sem("xt_ready")
        xt_hi_ready = sem("xt_hi_ready")
        xt_split = sem("xt_split")
        logits_ready = sem("logits_ready")
        logits_copied = sem("logits_copied")
        top_done = sem("top_done")
        ntop_ready = sem("ntop_ready")
        idx_done = sem("idx_done")
        m1_done = sem("m1_done")
        m12_done = sem("m12_done")
        el_ready = sem("el_ready")
        er_done = sem("er_done")
        w_ready = sem("w_ready")
        ffn_ready = sem("ffn_ready")
        acc_step = sem("acc_step")
        act_weighed = sem("act_weighed")
        pool_added = sem("pool_added")
        folded = sem("folded")
        banks_summed = sem("banks_summed")
        half_merged = sem("half_merged")
        acc_merged = sem("acc_merged")
        o_ready = sem("o_ready")

        block = ctx.enter_context(nc.Block())

        def in_dve(k):
            return k // EC * ND + sum(c < k % EC for c in DVE_CHUNKS)

        def banks_of_pool(j):
            return NA - SUMMED_BY_PE * (j == NT - 1)

        def in_act(k):
            return k - in_dve(k)

        def centre_wq(engine, wait_ge, n):
            w = slice(n * C // 2, (n + 1) * C // 2)
            wait_ge(wq_mean_done, n + 1)
            engine.tensor_tensor(wq_sb[:, w, :], wq_sb[:, w, :],
                                 wq_mean[:, w].unsqueeze(2).broadcast_to([P, C // 2, D]),
                                 ALU.subtract).then_inc(wq_ready[n], 1)

        def steps():
            for i in range(NT + LAG):
                yield (i, *(0 <= i - d < NT for d in (0, 1, 2, LAG)))

        @block.sync
        def _(sp):
            sp.dma_start(ctx_t[:, :, :], ctxT).then_inc(ld["ctx"], 16)
            for n in range(2):
                w = slice(n * C // 2, (n + 1) * C // 2)
                sp.dma_start(wq_sb[:, w, :], wqT[:, w, :]).then_inc(ld[f"wq{n}"], 16)
                if n == 0:
                    w = slice(H * DH // 2, H * DH)
                    sp.dma_start(wk_sb[:, w], wk[:, w]).then_inc(ld["wk1"], 16)
            sp.dma_start(xin_t[:, 0:4, :], xT[:, 0:4, :]).then_inc(ld["xT0"], 16)
            sp.dma_start(x_in[:, 0:4, :], x[:, 0:4, :]).then_inc(ld["x0"], 16)
            sp.dma_start(wv_sb[:, :], wv).then_inc(ld["wv"], 16)
            sp.dma_start(wo_sb[:, :, :], wo).then_inc(ld["wo"], 16)
            sp.dma_start(ident[:, :], ident_d).then_inc(ld["ident"], 16)
            sp.dma_start(sel_in[:, :], sel_d).then_inc(ld["sel"], 16)
            sp.dma_start(xin_t[:, 4:8, :], xT[:, 4:8, :]).then_inc(ld["xT1"], 16)
            sp.dma_start(x_in[:, 4:8, :], x[:, 4:8, :]).then_inc(ld["x1"], 16)
            sp.dma_start(iota[:, :], iota_d).then_inc(ld["iota"], 16)
            sp.dma_start(rw_sb[:, :], rwT).then_inc(ld["rw"], 16)
            for n in range(4):
                w = slice(n * E * D // 4, (n + 1) * E * D // 4)
                sp.dma_start(we_sb[:, w], we[:, w]).then_inc(ld[f"we{n}"], 16)
            for j in range(NT):
                sp.wait_ge(o_ready, j + 1)
                sp.dma_start(out[:, j, :], o_sb[:, j, :]).then_inc(out_stored, 16)
            sp.wait_ge(out_stored, 16 * NT)

        @block.tensor
        def _(pe):
            def fill(n):
                what, b, half = FILLS[n]
                ps = slot_ps[n % FB]
                if n >= FB:
                    pe.wait_ge(fill_act, n - FB + 1)
                    pe.wait_ge(fill_dve, dve_fills(n - FB + 1))
                if what == "K" and b == 0:
                    if half == 0:
                        pe.wait_ge(ld["ctx"], 16)
                    pe.wait_ge(ld[f"wk{half}"], 16)
                if what == "G":
                    n = FILLS.index(("K", b // 2 * 2, half)) + 1
                    pe.wait_ge(fill_act, n)
                    pe.wait_ge(fill_dve, dve_fills(n))
                if what == "G" and b == 0:
                    pe.wait_ge(wq_ready[half], 1)
                if what == "V" and b == 0 and half == 0:
                    pe.wait_ge(ld["wv"], 16)
                if what == "U":
                    n = FILLS.index(("V", b // 2 * 2, half)) + 1
                    pe.wait_ge(fill_act, n)
                    pe.wait_ge(fill_dve, dve_fills(n))
                if what == "U" and b == 0:
                    pe.wait_ge(ld["wo"], 16)
                for q in range(4):
                    c = 4 * half + q
                    if what in "KV":
                        w = wk_sb if what == "K" else wv_sb
                        lhs, rhs = w[:, c * P:(c + 1) * P], ctx_t[:, b:b + 2, :]
                    elif what == "G":
                        lhs, rhs = wq_sb[:, c, :], kt_bd[:, c, b, :]
                    else:
                        lhs, rhs = vt_bd[:, c, b, :], wo_sb[:, c, :]
                    mm = nc.tensor.matmul(ps[:, q * P:(q + 1) * P], lhs, rhs, start=True, stop=True)
                mm.then_inc(fill_ready, 1)

            def scores(i):
                b = i // TB
                if i:
                    pe.wait_ge(exp_done, i)
                if i % TB == 0:
                    pe.wait_ge(fill_dve, dve_fills(filled("G", b)))
                if i % 4 == 0:
                    pe.wait_ge(xin_lo_ready, i // 4 + 1)
                for s in range(2):
                    w = slice(s * BANK, (s + 1) * BANK)
                    nc.tensor.matmul(sim[:, w], xin_hi[:, i, :], g_hi[:, b, w], start=True, stop=False)
                    nc.tensor.matmul(sim[:, w], xin_hi[:, i, :], g_lo[:, b, w], start=False, stop=False)
                    mm = nc.tensor.matmul(sim[:, w], xin_lo[:, i, :], g_hi[:, b, w], start=False, stop=True)
                mm.then_inc(sim_ready, 1)

            def turn_max(i):
                pe.wait_ge(nmax_ready, i + 1)
                if i == 0:
                    pe.wait_ge(ld["ident"], 16)
                if i >= 2:
                    pe.wait_ge(logits_copied, i - 1)
                nc.tensor.transpose(maxT_ps, nmax_hl[:, i % 2, :].bitcast(F32), ident[:, :]).then_inc(nmaxT_ready, 1)

            def subtract_max(i):
                pe.wait_ge(nmaxT_copied, i + 1)
                if i == 0:
                    pe.wait_ge(sel_ready, 1)
                for s in range(2):
                    w = slice(s * BANK, (s + 1) * BANK)
                    mm = nc.tensor.matmul(sim[:, w], nmaxT[:, i % 2, :], sel[:, w], start=False, stop=True,
                                          skip_group_check=True)
                mm.then_inc(shifted, 1)

            def turn_attn(i, half):
                if half == 0:
                    pe.wait_ge(norm_done, i + 1)
                if 2 * i + half >= 1:
                    pe.wait_ge(attnT_copied, 2 * i + half)
                for q in range(4):
                    c = 4 * half + q
                    mm = nc.tensor.transpose(attn_ps[:, q * P:(q + 1) * P],
                                             prob[:, i % 2, 2 * c:2 * c + 2, :], ident[:, :])
                mm.then_inc(attnT_ready, 1)

            def attend(i):
                pe.wait_ge(attnT_copied, 2 * i + 2)
                if i:
                    pe.wait_ge(x1_done, i)
                if i % TB == 0:
                    pe.wait_ge(fill_act, filled("U", i // TB))
                for c in range(C):
                    mm = nc.tensor.matmul(av_ps, at[:, i % 2, c, :], u_sb[:, i // TB, c, :],
                                          start=(c == 0), stop=(c == C - 1))
                mm.then_inc(av_ready, 1)

            def turn_xn(i):
                pe.wait_ge(xn_ready, i + 1)
                if i + 1 < NT:
                    pe.wait_ge(nmaxT_copied, i + 2)
                if i:
                    pe.wait_ge(logits_copied, i)
                nc.tensor.transpose(xnT_ps, xn[:, i % 2, :], ident[:, :]).then_inc(xnT_ready, 1)

            def router(i):
                pe.wait_ge(xt_hi_ready, i + 1)
                if i == 0:
                    pe.wait_ge(ld["rw"], 16)
                nc.tensor.matmul(logits_ps, xt[:, i % 2, :], rw_sb[:, :], start=True, stop=True).then_inc(logits_ready, 1)

            def slot(i, c):
                if i < LAG:
                    return fill(EC * i + c)
                j = i - LAG
                if j >= NT:
                    return
                k = EC * j + c
                if c == 0:
                    pe.wait_ge(xt_split, j + 1)
                if k < EC and k % 2 == 0:
                    pe.wait_ge(we_lo_ready, k // 2 + 1)
                if k < FB:
                    n = len(FILLS) - FB + k + 1
                    pe.wait_ge(fill_act, n)
                    pe.wait_ge(fill_dve, dve_fills(n))
                elif (k - FB) % EC in DVE_CHUNKS:
                    pe.wait_ge(acc_step, EB * in_dve(k - FB + 1))
                else:
                    pe.wait_ge(act_weighed, in_act(k - FB + 1))
                o = slot_ps[k % FB][:, :]
                w = slice(c * BANK, (c + 1) * BANK)
                nc.tensor.matmul(o, xt_hi[:, j % 2, :], we_hi[:, w], start=True, stop=False)
                nc.tensor.matmul(o, xt_hi[:, j % 2, :], we_lo[:, w], start=False, stop=False)
                nc.tensor.matmul(o, xt_lo[:, j % 2, :], we_hi[:, w], start=False,
                                 stop=True).then_inc(ffn_ready, 1)

            def sum_banks():
                for n in range(NA * NT - SUMMED_BY_PE, NA * NT):
                    pe.wait_ge(act_weighed, n + 1)
                    for q in range(EB):
                        mm = nc.tensor.matmul(attn_ps[:, 0:D], ident[:, :], abuf[n % len(abuf)][:, q * D:(q + 1) * D],
                                              start=(n == NA * NT - SUMMED_BY_PE and q == 0),
                                              stop=(n == NA * NT - 1 and q == EB - 1))
                mm.then_inc(banks_summed, 1)

            for i, tile0, tile1, tile2, experts in steps():
                if i == 0:
                    pe.wait_ge(zeros_ready, 1)
                    for _ in range(WARM_UP):
                        nc.tensor.matmul(slot_ps[0][:, 0:P], zeros[:, :], zeros[:, :], start=True, stop=True)
                    slot(0, 0)
                    slot(0, 1)
                    slot(0, 2)
                    slot(0, 3)
                    slot(0, 4)
                    slot(0, 5)
                    scores(0)
                    slot(0, 6)
                    slot(0, 7)
                    turn_max(0)
                    continue
                if i == 1:
                    slot(1, 0)
                    subtract_max(0)
                    slot(1, 1)
                    slot(1, 2)
                    scores(1)
                    slot(1, 3)
                    slot(1, 4)
                    turn_attn(0, 0)
                    turn_max(1)
                    slot(1, 5)
                    turn_attn(0, 1)
                    subtract_max(1)
                    slot(1, 6)
                    attend(0)
                    slot(1, 7)
                    continue
                if i == 2:
                    slot(2, 0)
                    slot(2, 1)
                    scores(2)
                    turn_xn(0)
                    slot(2, 2)
                    slot(2, 3)
                    turn_attn(1, 0)
                    router(0)
                    slot(2, 4)
                    turn_attn(1, 1)
                    turn_max(2)
                    slot(2, 5)
                    subtract_max(2)
                    attend(1)
                    slot(2, 6)
                    slot(2, 7)
                    continue
                slot(i, 0)
                if tile0:
                    scores(i)
                if tile2:
                    turn_xn(i - 2)
                slot(i, 1)
                if tile1:
                    turn_attn(i - 1, 0)
                if tile2:
                    router(i - 2)
                slot(i, 2)
                if tile1:
                    turn_attn(i - 1, 1)
                if tile0:
                    turn_max(i)
                slot(i, 3)
                slot(i, 4)
                if tile0:
                    subtract_max(i)
                if tile1:
                    attend(i - 1)
                slot(i, 5)
                slot(i, 6)
                slot(i, 7)
            sum_banks()

        @block.vector
        def _(dve):
            def mean_wq(n):
                w = slice(n * C // 2, (n + 1) * C // 2)
                dve.wait_ge(ld[f"wq{n}"], 16)
                nc.vector.tensor_reduce(wq_sum[:, w], wq_sb[:, w, :], AX.X, ALU.add).then_inc(wq_summed, 1)
                dve.wait_ge(wq_summed, n + 1)
                nc.vector.tensor_scalar(wq_mean[:, w], wq_sum[:, w], 1.0 / D, None, ALU.mult).then_inc(wq_mean_done, 1)

            def variance_1(q):
                dve.wait_ge(ld[f"x{q}"], 16)
                for t in range(4 * q, 4 * q + 4):
                    nc.vector.bn_stats(st1[:, t, :], x_in[:, t, :]).then_inc(stats1, 1)
                for t in range(4 * q, 4 * q + 4):
                    dve.wait_ge(stats1, 4 * q + t + 1)
                    nc.vector.bn_aggr(mv1[:, t, :], st1[:, t, :]).then_inc(stats1, 1)
                dve.wait_ge(stats1, 8 * q + 8)
                nc.vector.tensor_scalar(ve1[:, 4 * q:4 * q + 4], mv1[:, 4 * q:4 * q + 4, 1], EPS, SCALE ** -2,
                                        ALU.add, ALU.mult).then_inc(ve1_ready, 1)

            def rest_x(q):
                dve.wait_ge(xin_hi_ready, q + 1)
                t = slice(4 * q, 4 * q + 4)
                nc.vector.tensor_tensor(xin_lo[:, t, :], xin_t[:, t, :], xin_hi[:, t, :].bitcast(F32),
                                        ALU.subtract).then_inc(xin_lo_ready, 1)

            def max_of(i):
                dve.wait_ge(sim_ready, i + 1)
                nc.vector.tensor_reduce(nmax[:, i % 2, :], sim[:, :].rearrange("p (h k) -> p h k", h=H),
                                        AX.X, ALU.max, negate=True).then_inc(nmax_done, 1)

            def max_hi(i):
                dve.wait_ge(nmax_done, i + 1)
                if i >= 2:
                    dve.wait_ge(nmaxT_ready, i - 1)
                nc.vector.tensor_copy(nmax_hl[:, i % 2, 0:H], nmax[:, i % 2, :]).then_inc(nmax_hi_done, 1)

            def max_lo(i):
                dve.wait_ge(nmax_hi_done, i + 1)
                nc.vector.tensor_tensor(nmax_hl[:, i % 2, H:2 * H], nmax[:, i % 2, :],
                                        nmax_hl[:, i % 2, 0:H].bitcast(F32), ALU.subtract).then_inc(nmax_ready, 1)

            def sum_of(i):
                dve.wait_ge(exp_done, i + 1)
                nc.vector.tensor_reduce(psum_h[:, i % 2, :], prob[:, i % 2, :, :], AX.X, ALU.add).then_inc(sum_done, 1)

            def sum_inverse(i):
                dve.wait_ge(sum_done, i + 1)
                if i >= 2:
                    dve.wait_ge(norm_done, i - 1)
                nc.vector.reciprocal(rsum_h[:, i % 2, :], psum_h[:, i % 2, :]).then_inc(rsum_ready, 1)

            def residual(i):
                dve.wait_ge(av_ready, i + 1)
                nc.vector.tensor_tensor(x1[:, i, :], av_ps, x_in[:, i, :], ALU.add).then_inc(x1_done, 1)

            def stats_2(i):
                dve.wait_ge(x1_done, i + 1)
                nc.vector.bn_stats(st2[:, i, :], x1[:, i, :]).then_inc(stats2, 1)

            def aggregate_2(i):
                dve.wait_ge(stats2, 2 * i + 1)
                nc.vector.bn_aggr(mv2[:, i, :], st2[:, i, :]).then_inc(stats2, 1)

            def variance_2(i):
                dve.wait_ge(stats2, 2 * i + 2)
                nc.vector.tensor_scalar(ve2[:, i:i + 1], mv2[:, i, 1:2], EPS, None, ALU.add).then_inc(ve2_ready, 1)

            def apply_norm_2(i):
                dve.wait_ge(rstd2_ready, i + 1)
                if i >= 2:
                    dve.wait_ge(xnT_ready, i - 1)
                nc.vector.tensor_scalar(xn[:, i % 2, :], x1[:, i, :], mv2[:, i, 0:1], rstd2[:, i:i + 1],
                                        ALU.subtract, ALU.mult).then_inc(xn_ready, 1)

            def rest_xt(i):
                dve.wait_ge(xt_hi_ready, i + 1)
                if i >= 2:
                    dve.wait_ge(ffn_ready, EC * (i - 1))
                nc.vector.tensor_tensor(xt_lo[:, i % 2, :], xt[:, i % 2, :], xt_hi[:, i % 2, :].bitcast(F32),
                                        ALU.subtract).then_inc(xt_split, 1)

            def top_values(i):
                dve.wait_ge(logits_copied, i + 1)
                nc.vector.max(top8[:, i % 2, :], lg[:, i % 2, :]).then_inc(top_done, 1)

            def minus_top(i):
                dve.wait_ge(top_done, i + 1)
                nc.vector.tensor_scalar(ntop[:, i % 2, :], top8[:, i % 2, 0:1], -1.0, None, ALU.mult).then_inc(ntop_ready, 1)

            def top_places(i):
                nc.vector.max_index(idx8[:, i % 2, :], top8[:, i % 2, :], lg[:, i % 2, :]).then_inc(idx_done, 1)

            def mask_first(i):
                dve.wait_ge(idx_done, i + 1)
                nc.vector.tensor_scalar(m1[:, i % 2, :], iota[:, :], idx8[:, i % 2, 0:1], None,
                                        ALU.is_equal).then_inc(m1_done, 1)

            def mask_both(i):
                dve.wait_ge(m1_done, i + 1)
                nc.vector.scalar_tensor_tensor(m12[:, i % 2, :], iota[:, :], idx8[:, i % 2, 1:2], m1[:, i % 2, :],
                                               ALU.is_equal, ALU.add).then_inc(m12_done, 1)

            def weight_scale(i):
                dve.wait_ge(el_ready, i + 1)
                nc.vector.reciprocal(er[:, i % 2, :], es[:, i % 2, :]).then_inc(er_done, 1)

            def weights(i):
                p = i % 2
                dve.wait_ge(er_done, i + 1)
                dve.wait_ge(m12_done, i + 1)
                if i >= 2:
                    dve.wait_ge(act_weighed, NA * (i - 1))
                nc.vector.scalar_tensor_tensor(wt[:, p, :], el[:, p, :], er[:, p, 0:1], m12[:, p, :],
                                               ALU.mult, ALU.mult).then_inc(w_ready, 1)

            def slot(i, c, *quarters):
                if i < LAG:
                    if 0 in quarters:
                        fill(EC * i + c)
                    return
                j = i - LAG
                if j >= NT or c not in DVE_CHUNKS:
                    return
                k = EC * j + c
                for q in quarters:
                    n = EB * in_dve(k) + q
                    first = n - EB * in_dve(EC * j)
                    if q == 0:
                        dve.wait_ge(ffn_ready, k + 1)
                    if first == 0:
                        dve.wait_ge(w_ready, j + 1)
                        if j >= 2:
                            dve.wait_ge(acc_merged, j - 1)
                    if first >= 2:
                        dve.wait_ge(acc_step, n - 1)
                    y = slot_ps[k % FB][:, q * D:(q + 1) * D]
                    w = wt[:, j % 2, EB * c + q:EB * c + q + 1]
                    if first == 1:
                        ins = nc.vector.tensor_scalar(acc[:, j % 2, 1, :], y, w, None, ALU.mult)
                    else:
                        chain = acc[:, j % 2, n % 2, :]
                        before = x1[:, j, :] if first == 0 else chain
                        ins = nc.vector.scalar_tensor_tensor(chain, y, w, before, ALU.mult, ALU.add)
                    ins.then_inc(acc_step, 1)

            def merge(j):
                dve.wait_ge(folded, 2 * j + 2)
                dve.wait_ge(acc_step, EB * ND * (j + 1) - 1)
                nc.vector.tensor_tensor(psum2[:, 1, :], psum2[:, 0, :], acc[:, j % 2, 0, :],
                                        ALU.add).then_inc(acc_merged, 1)
                dve.wait_ge(acc_step, EB * ND * (j + 1))
                rest = acc[:, j % 2, 1, :]
                if j == NT - 1:
                    dve.wait_ge(banks_summed, 1)
                    nc.vector.tensor_tensor(pfold[:, 0:D], attn_ps[:, 0:D], rest, ALU.add).then_inc(half_merged, 1)
                    dve.wait_ge(half_merged, 1)
                    rest = pfold[:, 0:D]
                dve.wait_ge(acc_merged, j + 1)
                nc.vector.tensor_tensor(o_sb[:, j, :], psum2[:, 1, :], rest, ALU.add).then_inc(o_ready, 1)

            def fill(n):
                what, b, half = FILLS[n]
                ps = slot_ps[n % FB]
                c = slice(4 * half, 4 * half + 4)
                if what in "KV":
                    dst = kt_bd if what == "K" else vt_bd
                    dve.wait_ge(fill_ready, n + 1)
                    nc.vector.tensor_copy(dst[M:P, c, b:b + 2, M:2 * M],
                                          ps[M:P, :].rearrange("p (c b k) -> p c b k", c=4, b=2)
                                          ).then_inc(fill_dve, 1)
                if what == "G":
                    w = slice(half * BANK, (half + 1) * BANK)
                    dve.wait_ge(fill_act, n + 1)
                    nc.vector.tensor_tensor(g_lo[:, b, w], ps[:, :], g_hi[:, b, w].bitcast(F32),
                                            ALU.subtract).then_inc(fill_dve, 1)

            def round_experts(n):
                dve.wait_ge(ld[f"we{n}"], 16)
                w = slice(n * E * D // 4, (n + 1) * E * D // 4)
                nc.vector.tensor_copy(we_hi[:, w], we_sb[:, w]).then_inc(we_hi_ready, 1)

            for i, tile0, tile1, tile2, experts in steps():
                if i == 0:
                    nc.vector.memset(zeros[:, :], 0.0).then_inc(zeros_ready, 1)
                    nc.vector.memset(vt_bd[M:P, :, :, 0:M], 0.0)
                    mean_wq(0)
                    centre_wq(nc.vector, dve.wait_ge, 0)
                    mean_wq(1)
                    slot(0, 0, 0)
                    slot(0, 1, 0)
                    variance_1(0)
                    rest_x(0)
                    slot(0, 2, 0)
                    slot(0, 3, 0)
                    slot(0, 4, 0)
                    slot(0, 5, 0)
                    max_of(0)
                    max_hi(0)
                    max_lo(0)
                    continue
                if i == 1:
                    slot(1, 0, 0)
                    slot(1, 1, 0)
                    sum_of(0)
                    sum_inverse(0)
                    slot(1, 2, 0)
                    max_of(1)
                    max_hi(1)
                    max_lo(1)
                    slot(1, 3, 0)
                    slot(1, 4, 0)
                    variance_1(1)
                    round_experts(0)
                    slot(1, 5, 0)
                    sum_of(1)
                    sum_inverse(1)
                    residual(0)
                    stats_2(0)
                    round_experts(1)
                    aggregate_2(0)
                    variance_2(0)
                    rest_x(1)
                    apply_norm_2(0)
                    continue
                if i == 2:
                    slot(2, 0, 0)
                    slot(2, 1, 0)
                    max_of(2)
                    max_hi(2)
                    max_lo(2)
                    rest_xt(0)
                    dve.wait_ge(ld["iota"], 16)
                    top_values(0)
                    minus_top(0)
                    top_places(0)
                    mask_first(0)
                    mask_both(0)
                    slot(2, 4, 0)
                    slot(2, 5, 0)
                    sum_of(2)
                    residual(1)
                    sum_inverse(2)
                    stats_2(1)
                    round_experts(2)
                    aggregate_2(1)
                    variance_2(1)
                    weight_scale(0)
                    weights(0)
                    apply_norm_2(1)
                    round_experts(3)
                    continue
                slot(i, 0, 0, 1, 2, 3)
                if tile0:
                    max_of(i)
                slot(i, 1, 0)
                if tile0:
                    max_hi(i)
                slot(i, 1, 1)
                if tile0:
                    max_lo(i)
                if tile2:
                    rest_xt(i - 2)
                slot(i, 1, 2)
                if tile2:
                    top_values(i - 2)
                    minus_top(i - 2)
                    top_places(i - 2)
                slot(i, 1, 3)
                slot(i, 2, 0, 1, 2, 3)
                if tile2:
                    mask_first(i - 2)
                slot(i, 3, 0)
                if tile2:
                    mask_both(i - 2)
                slot(i, 3, 1, 2, 3)
                if NT - DVE_MERGED < i - LAG < NT:
                    merge(i - LAG - 1)
                if tile0:
                    sum_of(i)
                if tile1:
                    residual(i - 1)
                if tile0:
                    sum_inverse(i)
                if tile1:
                    stats_2(i - 1)
                slot(i, 4, 0, 1, 2, 3)
                slot(i, 5, 0)
                if tile1:
                    aggregate_2(i - 1)
                slot(i, 5, 1)
                if tile1:
                    variance_2(i - 1)
                slot(i, 5, 2)
                if tile2:
                    weight_scale(i - 2)
                slot(i, 5, 3)
                if tile2:
                    weights(i - 2)
                slot(i, 6, 0, 1, 2, 3)
                if tile1:
                    apply_norm_2(i - 1)
                slot(i, 7, 0, 1, 2, 3)
                if i - LAG == NT - 1:
                    merge(NT - 1)

        @block.scalar
        def _(act):
            w = slice(0, H * DH // 2)
            act.dma_start(wk_sb[:, w], wk[:, w]).then_inc(ld["wk0"], 16)

            def round_x(q):
                act.wait_ge(ld[f"xT{q}"], 16)
                nc.scalar.activation(xin_hi[:, 4 * q:4 * q + 4, :], xin_t[:, 4 * q:4 * q + 4, :],
                                     ACT.Copy).then_inc(xin_hi_ready, 1)

            def copy_maxT(i):
                act.wait_ge(nmaxT_ready, i + 1)
                if i >= 2:
                    act.wait_ge(shifted, i - 1)
                nc.scalar.activation(nmaxT[:, i % 2, :], maxT_ps, ACT.Copy).then_inc(nmaxT_copied, 1)

            def exponentials(i):
                act.wait_ge(shifted, i + 1)
                act.wait_ge(rstd1_ready, i // 4 + 1)
                if i >= 2:
                    act.wait_ge(attnT_ready, 2 * (i - 1))
                nc.scalar.activation(prob[:, i % 2, :, :], sim[:, :].rearrange("p (h k) -> p h k", h=H),
                                     ACT.Exp, scale=rstd1[:, i:i + 1]).then_inc(exp_done, 1)

            def copy_attnT(i, half):
                act.wait_ge(attnT_ready, 2 * i + half + 1)
                if i >= 2:
                    act.wait_ge(av_ready, i - 1)
                nc.scalar.activation(at[:, i % 2, 4 * half:4 * half + 4, :],
                                     attn_ps[:, :].rearrange("p (c n) -> p c n", c=4),
                                     ACT.Copy).then_inc(attnT_copied, 1)

            def copy_xnT(i):
                act.wait_ge(xnT_ready, i + 1)
                if i >= 2:
                    act.wait_ge(xt_split, i - 1)
                    act.wait_ge(logits_ready, i - 1)
                    act.wait_ge(ffn_ready, EC * (i - 1))
                nc.scalar.activation(xt[:, i % 2, :], xnT_ps, ACT.Copy).then_inc(xt_ready, 1)
                nc.scalar.activation(xt_hi[:, i % 2, :], xnT_ps, ACT.Copy).then_inc(xt_hi_ready, 1)

            def copy_logits(i):
                act.wait_ge(logits_ready, i + 1)
                if i >= 2:
                    act.wait_ge(idx_done, i - 1)
                nc.scalar.activation(lg[:, i % 2, :], logits_ps, ACT.Copy).then_inc(logits_copied, 1)

            def router_exp(i):
                act.wait_ge(ntop_ready, i + 1)
                act.wait_ge(logits_copied, i + 1)
                if i >= 2:
                    act.wait_ge(w_ready, i - 1)
                nc.scalar.activation(el[:, i % 2, :], lg[:, i % 2, :], ACT.Exp, bias=ntop[:, i % 2, 0:1],
                                     accum_out=es[:, i % 2, 0:1]).then_inc(el_ready, 1)

            def slot(i, c):
                if i < LAG:
                    return fill(EC * i + c)
                j = i - LAG
                if j >= NT or c in DVE_CHUNKS:
                    return
                k = EC * j + c
                n = in_act(k)
                act.wait_ge(ffn_ready, k + 1)
                act.wait_ge(w_ready, j + 1)
                if n >= len(abuf):
                    before = n - len(abuf)
                    act.wait_ge(pool_added, (NA - 1) * (before // NA) + max(before % NA, 1))
                for q in range(EB):
                    e = EB * c + q
                    ins = nc.scalar.activation(abuf[n % len(abuf)][:, q * D:(q + 1) * D],
                                               slot_ps[k % FB][:, q * D:(q + 1) * D], ACT.Copy,
                                               scale=wt[:, j % 2, e:e + 1])
                ins.then_inc(act_weighed, 1)

            def fill(n):
                what, b, half = FILLS[n]
                ps = slot_ps[n % FB]
                c = slice(4 * half, 4 * half + 4)
                w = slice(half * BANK, (half + 1) * BANK)
                if n == 0:
                    act.wait_ge(zeroed, 3)
                if n == FILLS.index(("V", 0, 0)):
                    act.wait_ge(zeroed, 4)
                act.wait_ge(fill_ready, n + 1)
                if what in "KV":
                    dst = kt_bd if what == "K" else vt_bd
                    ins = nc.scalar.activation(dst[0:M, c, b:b + 2, 0:M],
                                               ps[0:M, :].rearrange("p (c b k) -> p c b k", c=4, b=2), ACT.Copy)
                elif what == "G":
                    ins = nc.scalar.activation(g_hi[:, b, w], ps[:, :], ACT.Copy)
                else:
                    ins = nc.scalar.activation(u_sb[:, b, c, :], ps[:, :].rearrange("p (c d) -> p c d", c=4), ACT.Copy)
                ins.then_inc(fill_act, 1)

            act.wait_ge(zeroed, 1)
            nc.scalar.activation(warm[:, :], mhalf[:, 0:1], ACT.Exp)
            for i, tile0, tile1, tile2, experts in steps():
                if i == 0:
                    slot(0, 0)
                    slot(0, 1)
                    round_x(0)
                    slot(0, 2)
                    slot(0, 3)
                    slot(0, 4)
                    slot(0, 5)
                    act.wait_ge(ld["sel"], 16)
                    nc.scalar.activation(sel[:, :], sel_in[:, :], ACT.Copy).then_inc(sel_ready, 1)
                    slot(0, 6)
                    slot(0, 7)
                    copy_maxT(0)
                    continue
                if i == 1:
                    slot(1, 0)
                    exponentials(0)
                    slot(1, 1)
                    slot(1, 2)
                    slot(1, 3)
                    slot(1, 4)
                    copy_attnT(0, 0)
                    copy_maxT(1)
                    slot(1, 5)
                    copy_attnT(0, 1)
                    exponentials(1)
                    slot(1, 6)
                    round_x(1)
                    slot(1, 7)
                    continue
                if i == 2:
                    slot(2, 0)
                    slot(2, 1)
                    copy_xnT(0)
                    slot(2, 2)
                    slot(2, 3)
                    copy_attnT(1, 0)
                    copy_logits(0)
                    slot(2, 4)
                    copy_attnT(1, 1)
                    copy_maxT(2)
                    slot(2, 5)
                    exponentials(2)
                    router_exp(0)
                    slot(2, 6)
                    slot(2, 7)
                    continue
                if tile2:
                    copy_xnT(i - 2)
                if tile1:
                    copy_attnT(i - 1, 0)
                if tile2:
                    copy_logits(i - 2)
                slot(i, 0)
                slot(i, 1)
                if tile1:
                    copy_attnT(i - 1, 1)
                if tile0:
                    copy_maxT(i)
                slot(i, 2)
                slot(i, 3)
                if tile0:
                    exponentials(i)
                if tile2:
                    router_exp(i - 2)
                slot(i, 4)
                slot(i, 5)
                slot(i, 6)
                slot(i, 7)

        @block.gpsimd
        def _(pool):
            nc.gpsimd.memset(mhalf[:, :], -0.5).then_inc(zeroed, 1)
            pool.wait_ge(zeroed, 1)
            nc.gpsimd.memset(kt_bd[0:M, :, :, M:2 * M], 0.0).then_inc(zeroed, 1)
            pool.wait_ge(zeroed, 2)
            nc.gpsimd.memset(kt_bd[M:P, :, :, 0:M], 0.0).then_inc(zeroed, 1)
            pool.wait_ge(zeroed, 3)

            def rstd_1(q):
                pool.wait_ge(ve1_ready, q + 1)
                nc.gpsimd.tensor_tensor(rstd1[:, 4 * q:4 * q + 4], ve1[:, 4 * q:4 * q + 4], mhalf[:, 0:4],
                                        ALU.pow).then_inc(rstd1_ready, 1)

            def rest_experts(n):
                pool.wait_ge(we_hi_ready, n + 1)
                w = slice(n * E * D // 4, (n + 1) * E * D // 4)
                nc.gpsimd.tensor_tensor(we_lo[:, w], we_sb[:, w], we_hi[:, w].bitcast(F32),
                                        ALU.subtract).then_inc(we_lo_ready, 1)

            def normalise_probs(i):
                pool.wait_ge(rsum_ready, i + 1)
                nc.gpsimd.tensor_tensor(prob[:, i % 2, :, :], prob[:, i % 2, :, :],
                                        rsum_h[:, i % 2, :].unsqueeze(2).broadcast_to([P, H, M]),
                                        ALU.mult).then_inc(norm_done, 1)

            def rstd_2(i):
                pool.wait_ge(ve2_ready, i + 1)
                nc.gpsimd.tensor_tensor(rstd2[:, i:i + 1], ve2[:, i:i + 1], mhalf[:, 0:1],
                                        ALU.pow).then_inc(rstd2_ready, 1)

            def slot(i, c):
                j = i - LAG
                if not 0 <= j < NT or c in DVE_CHUNKS:
                    return
                n = in_act(EC * j + c)
                m = n % NA
                if m >= banks_of_pool(j):
                    return
                if m == 0:
                    return
                pool.wait_ge(act_weighed, n + 1)
                if m == 1:
                    before = abuf[(n - 1) % len(abuf)]
                else:
                    pool.wait_ge(pool_added, (NA - 1) * j + m - 1)
                    before = pacc[:, m % 2, :]
                nc.gpsimd.tensor_tensor(pacc[:, (m + 1) % 2, :], before, abuf[n % len(abuf)],
                                        ALU.add).then_inc(pool_added, 1)

            def fold(j):
                banks = banks_of_pool(j)
                pool.wait_ge(pool_added, (NA - 1) * j + banks - 1)
                a = pacc[:, banks % 2, :]
                nc.gpsimd.tensor_tensor(pfold[:, :], a[:, 0:2 * D], a[:, 2 * D:4 * D], ALU.add).then_inc(folded, 1)
                pool.wait_ge(folded, 2 * j + 1)
                if j > NT - DVE_MERGED:
                    pool.wait_ge(acc_merged, j)
                nc.gpsimd.tensor_tensor(psum2[:, 0, :], pfold[:, 0:D], pfold[:, D:2 * D], ALU.add).then_inc(folded, 1)

            def merge(j):
                pool.wait_ge(acc_step, EB * ND * (j + 1))
                nc.gpsimd.tensor_tensor(psum2[:, 1, :], acc[:, j % 2, 0, :], acc[:, j % 2, 1, :], ALU.add).then_inc(acc_merged, 1)
                pool.wait_ge(acc_merged, j + 1)
                pool.wait_ge(folded, 2 * j + 2)
                nc.gpsimd.tensor_tensor(o_sb[:, j, :], psum2[:, 0, :], psum2[:, 1, :], ALU.add).then_inc(o_ready, 1)

            nc.gpsimd.memset(vt_bd[0:M, :, :, M:2 * M], 0.0).then_inc(zeroed, 1)
            pool.wait_ge(zeroed, 4)
            centre_wq(nc.gpsimd, pool.wait_ge, 1)
            rstd_1(0)
            for i, tile0, tile1, tile2, experts in steps():
                slot(i, 0)
                slot(i, 1)
                slot(i, 2)
                slot(i, 3)
                if tile1:
                    rstd_2(i - 1)
                if tile0:
                    normalise_probs(i)
                if i < LAG:
                    rest_experts(i)
                if i == 1:
                    rstd_1(1)
                slot(i, 4)
                slot(i, 5)
                slot(i, 6)
                slot(i, 7)
                if i == LAG - 1:
                    rest_experts(LAG)
                if experts:
                    fold(i - LAG)
                    if i - LAG < NT - DVE_MERGED:
                        merge(i - LAG)


_OUT = (B, N, D)


def kernel(**inputs):
    import concourse.bacc as _bacc
    from concourse.bass_utils import run_bass_kernel_spmd as _run

    a = {k: np.asarray(v) for k, v in inputs.items()}
    laid = {
        "x": a["x"].reshape(NT, P, D).transpose(1, 0, 2),
        "xT": a["x"].reshape(NT, P, D).transpose(2, 0, 1),
        "ctxT": a["ctx_1024"].transpose(2, 0, 1),
        "wk": a["L0_xattn_Wk"],
        "wqT": a["L0_xattn_Wq"].T.reshape(C, P, D).transpose(1, 0, 2),
        "wv": a["L0_xattn_Wv"],
        "wo": a["L0_xattn_Wo"].reshape(C, P, D).transpose(1, 0, 2),
        "rwT": a["L0_ffn_router_w"].T,
        "we": a["L0_ffn_expert_weights"].transpose(1, 0, 2).reshape(D, E * D),
        "ident": np.eye(P, dtype=np.float32),
        "sel": np.tile(np.repeat(np.eye(H, dtype=np.float32), M, axis=1), (2, 1)),
        "iota": np.tile(np.arange(E, dtype=np.float32), (P, 1)),
    }
    nc = _bacc.Bacc("TRN2", target_bir_lowering=False, num_devices=1)
    arrays, args = {}, []
    for name, v in laid.items():
        v = np.ascontiguousarray(v)
        arrays[f"in_{name}"] = v
        args.append(nc.dram_tensor(f"in_{name}", v.shape, mybir.dt.from_np(v.dtype), kind="ExternalInput").ap())
    args.append(nc.dram_tensor("out_0", (P, NT, D), F32, kind="ExternalOutput").ap())
    build(nc, *args)
    r = _run(nc, [arrays], core_ids=[0])
    got = r.results[0]["out_0"]
    return got.transpose(1, 0, 2).reshape(_OUT)
```
